# Optimizing a Trainium2 kernel written in Bass

```python
import numpy as np
import jax
import jax.numpy as jnp

def _softmax(x, axis=-1):
    return jax.nn.softmax(x, axis=axis)

def _gelu(x):
    return jax.nn.gelu(x, approximate=True)

def _silu(x):
    return jax.nn.silu(x)

def _sigmoid(x):
    return jax.nn.sigmoid(x)

def _layernorm(x, axis=-1, eps=1e-05):
    m = jnp.mean(x, axis=axis, keepdims=True)
    v = jnp.var(x, axis=axis, keepdims=True)
    return (x - m) / jnp.sqrt(v + eps)

def _scatter_add(tgt, idx, src, axis=0):
    return tgt.at[idx].add(src)

def _segment_sum(src, seg, n):
    return jax.ops.segment_sum(src, seg, n)
kernel_name = 'mk_dlrm_tower_d1_rec_r8_974bc6'

def setup_inputs(seed: int=0):
    np.random.seed(seed)
    _w = jnp.asarray

    def _rec_inputs():
        import jax
        import jax.numpy as jnp
        _tk = jax.random.key(seed)
        dense_ctx = jax.random.normal(jax.random.fold_in(_tk, 190), (1024, 16), jnp.float32)
        ids = jnp.stack([jax.random.randint(jax.random.fold_in(_tk, 200 + f), (1024,), 0, v, jnp.int32) for f, v in enumerate([125000, 1000, 1250, 1000, 1250, 12500, 1250, 12500, 1250, 1000, 1000, 1000, 1250, 1250, 125000, 125000, 12500, 1000, 12500, 1000, 1000, 1000, 1000, 12500, 12500, 12500, 1250, 1250, 1000, 1250, 1000, 1250])], axis=1)
        tbl_0 = 0.05 * jax.random.normal(jax.random.fold_in(_tk, 500 + 0), (125000, 64), jnp.float32)
        tbl_1 = 0.05 * jax.random.normal(jax.random.fold_in(_tk, 500 + 1), (1000, 64), jnp.float32)
        tbl_2 = 0.05 * jax.random.normal(jax.random.fold_in(_tk, 500 + 2), (1250, 64), jnp.float32)
        tbl_3 = 0.05 * jax.random.normal(jax.random.fold_in(_tk, 500 + 3), (1000, 64), jnp.float32)
        tbl_4 = 0.05 * jax.random.normal(jax.random.fold_in(_tk, 500 + 4), (1250, 64), jnp.float32)
        tbl_5 = 0.05 * jax.random.normal(jax.random.fold_in(_tk, 500 + 5), (12500, 64), jnp.float32)
        tbl_6 = 0.05 * jax.random.normal(jax.random.fold_in(_tk, 500 + 6), (1250, 64), jnp.float32)
        tbl_7 = 0.05 * jax.random.normal(jax.random.fold_in(_tk, 500 + 7), (12500, 64), jnp.float32)
        tbl_8 = 0.05 * jax.random.normal(jax.random.fold_in(_tk, 500 + 8), (1250, 64), jnp.float32)
        tbl_9 = 0.05 * jax.random.normal(jax.random.fold_in(_tk, 500 + 9), (1000, 64), jnp.float32)
        tbl_10 = 0.05 * jax.random.normal(jax.random.fold_in(_tk, 500 + 10), (1000, 64), jnp.float32)
        tbl_11 = 0.05 * jax.random.normal(jax.random.fold_in(_tk, 500 + 11), (1000, 64), jnp.float32)
        tbl_12 = 0.05 * jax.random.normal(jax.random.fold_in(_tk, 500 + 12), (1250, 64), jnp.float32)
        tbl_13 = 0.05 * jax.random.normal(jax.random.fold_in(_tk, 500 + 13), (1250, 64), jnp.float32)
        tbl_14 = 0.05 * jax.random.normal(jax.random.fold_in(_tk, 500 + 14), (125000, 64), jnp.float32)
        tbl_15 = 0.05 * jax.random.normal(jax.random.fold_in(_tk, 500 + 15), (125000, 64), jnp.float32)
        tbl_16 = 0.05 * jax.random.normal(jax.random.fold_in(_tk, 500 + 16), (12500, 64), jnp.float32)
        tbl_17 = 0.05 * jax.random.normal(jax.random.fold_in(_tk, 500 + 17), (1000, 64), jnp.float32)
        tbl_18 = 0.05 * jax.random.normal(jax.random.fold_in(_tk, 500 + 18), (12500, 64), jnp.float32)
        tbl_19 = 0.05 * jax.random.normal(jax.random.fold_in(_tk, 500 + 19), (1000, 64), jnp.float32)
        tbl_20 = 0.05 * jax.random.normal(jax.random.fold_in(_tk, 500 + 20), (1000, 64), jnp.float32)
        tbl_21 = 0.05 * jax.random.normal(jax.random.fold_in(_tk, 500 + 21), (1000, 64), jnp.float32)
        tbl_22 = 0.05 * jax.random.normal(jax.random.fold_in(_tk, 500 + 22), (1000, 64), jnp.float32)
        tbl_23 = 0.05 * jax.random.normal(jax.random.fold_in(_tk, 500 + 23), (12500, 64), jnp.float32)
        tbl_24 = 0.05 * jax.random.normal(jax.random.fold_in(_tk, 500 + 24), (12500, 64), jnp.float32)
        tbl_25 = 0.05 * jax.random.normal(jax.random.fold_in(_tk, 500 + 25), (12500, 64), jnp.float32)
        tbl_26 = 0.05 * jax.random.normal(jax.random.fold_in(_tk, 500 + 26), (1250, 64), jnp.float32)
        tbl_27 = 0.05 * jax.random.normal(jax.random.fold_in(_tk, 500 + 27), (1250, 64), jnp.float32)
        tbl_28 = 0.05 * jax.random.normal(jax.random.fold_in(_tk, 500 + 28), (1000, 64), jnp.float32)
        tbl_29 = 0.05 * jax.random.normal(jax.random.fold_in(_tk, 500 + 29), (1250, 64), jnp.float32)
        tbl_30 = 0.05 * jax.random.normal(jax.random.fold_in(_tk, 500 + 30), (1000, 64), jnp.float32)
        tbl_31 = 0.05 * jax.random.normal(jax.random.fold_in(_tk, 500 + 31), (1250, 64), jnp.float32)
        _rk = jax.random.fold_in(_tk, 7)
        W_top1 = 0.0428746 * jax.random.normal(jax.random.fold_in(_tk, 801), (544, 512), jnp.float32)
        W_top2 = 0.0441942 * jax.random.normal(jax.random.fold_in(_tk, 802), (512, 256), jnp.float32)
        W_top3 = 0.0625 * jax.random.normal(jax.random.fold_in(_tk, 803), (256, 1), jnp.float32)
        b_top1 = jnp.zeros((512,), jnp.float32)
        b_top2 = jnp.zeros((256,), jnp.float32)
        return (dense_ctx, ids, tbl_0, tbl_1, tbl_2, tbl_3, tbl_4, tbl_5, tbl_6, tbl_7, tbl_8, tbl_9, tbl_10, tbl_11, tbl_12, tbl_13, tbl_14, tbl_15, tbl_16, tbl_17, tbl_18, tbl_19, tbl_20, tbl_21, tbl_22, tbl_23, tbl_24, tbl_25, tbl_26, tbl_27, tbl_28, tbl_29, tbl_30, tbl_31, W_top1, b_top1, W_top2, b_top2, W_top3)
    dense_ctx, ids, tbl_0, tbl_1, tbl_2, tbl_3, tbl_4, tbl_5, tbl_6, tbl_7, tbl_8, tbl_9, tbl_10, tbl_11, tbl_12, tbl_13, tbl_14, tbl_15, tbl_16, tbl_17, tbl_18, tbl_19, tbl_20, tbl_21, tbl_22, tbl_23, tbl_24, tbl_25, tbl_26, tbl_27, tbl_28, tbl_29, tbl_30, tbl_31, W_top1, b_top1, W_top2, b_top2, W_top3 = _rec_inputs()

    def _L0_rec_setup():
        import jax, jax.numpy as jnp
        import numpy as np
        B, F, D = (512, 32, 64)
        II, JJ = np.triu_indices(F, k=1)
        P = II.shape[0]
        key = jax.random.key(seed)
        kx, kk = jax.random.split(key)
        x = jax.random.normal(kx, (B, F, D), dtype=jnp.float32)
        kernels = jax.random.normal(kk, (P, D, D), dtype=jnp.float32) * 0.001
        return {'x': x, 'kernels': kernels}
    _L0_rec_all = _L0_rec_setup()
    _L0_rec_in = {k: v for k, v in _L0_rec_all.items() if k in ('kernels',)}
    del _L0_rec_all
    return {'dense_ctx': dense_ctx, 'ids': ids, 'tbl_0': tbl_0, 'tbl_1': tbl_1, 'tbl_2': tbl_2, 'tbl_3': tbl_3, 'tbl_4': tbl_4, 'tbl_5': tbl_5, 'tbl_6': tbl_6, 'tbl_7': tbl_7, 'tbl_8': tbl_8, 'tbl_9': tbl_9, 'tbl_10': tbl_10, 'tbl_11': tbl_11, 'tbl_12': tbl_12, 'tbl_13': tbl_13, 'tbl_14': tbl_14, 'tbl_15': tbl_15, 'tbl_16': tbl_16, 'tbl_17': tbl_17, 'tbl_18': tbl_18, 'tbl_19': tbl_19, 'tbl_20': tbl_20, 'tbl_21': tbl_21, 'tbl_22': tbl_22, 'tbl_23': tbl_23, 'tbl_24': tbl_24, 'tbl_25': tbl_25, 'tbl_26': tbl_26, 'tbl_27': tbl_27, 'tbl_28': tbl_28, 'tbl_29': tbl_29, 'tbl_30': tbl_30, 'tbl_31': tbl_31, 'W_top1': W_top1, 'b_top1': b_top1, 'W_top2': W_top2, 'b_top2': b_top2, 'W_top3': W_top3, 'L0_rec_kernels': _L0_rec_in['kernels']}

def reference(dense_ctx, ids, tbl_0, tbl_1, tbl_2, tbl_3, tbl_4, tbl_5, tbl_6, tbl_7, tbl_8, tbl_9, tbl_10, tbl_11, tbl_12, tbl_13, tbl_14, tbl_15, tbl_16, tbl_17, tbl_18, tbl_19, tbl_20, tbl_21, tbl_22, tbl_23, tbl_24, tbl_25, tbl_26, tbl_27, tbl_28, tbl_29, tbl_30, tbl_31, W_top1, b_top1, W_top2, b_top2, W_top3, L0_rec_kernels):
    import jax
    import jax.numpy as jnp

    def _L0_rec_ref(x, kernels):
        import jax, jax.numpy as jnp
        import numpy as np
        B, F, D = (512, 32, 64)
        II, JJ = np.triu_indices(F, k=1)
        P = II.shape[0]
        z = jnp.sum(x, axis=-1)
        xi = x[:, II, :]
        xj = x[:, JJ, :]
        outer = jnp.einsum('bpd,pde,bpe->bp', xi, kernels, xj)
        return jnp.concatenate([z, outer], axis=1)
    e = jnp.stack([tbl_0[ids[:, 0]], tbl_1[ids[:, 1]], tbl_2[ids[:, 2]], tbl_3[ids[:, 3]], tbl_4[ids[:, 4]], tbl_5[ids[:, 5]], tbl_6[ids[:, 6]], tbl_7[ids[:, 7]], tbl_8[ids[:, 8]], tbl_9[ids[:, 9]], tbl_10[ids[:, 10]], tbl_11[ids[:, 11]], tbl_12[ids[:, 12]], tbl_13[ids[:, 13]], tbl_14[ids[:, 14]], tbl_15[ids[:, 15]], tbl_16[ids[:, 16]], tbl_17[ids[:, 17]], tbl_18[ids[:, 18]], tbl_19[ids[:, 19]], tbl_20[ids[:, 20]], tbl_21[ids[:, 21]], tbl_22[ids[:, 22]], tbl_23[ids[:, 23]], tbl_24[ids[:, 24]], tbl_25[ids[:, 25]], tbl_26[ids[:, 26]], tbl_27[ids[:, 27]], tbl_28[ids[:, 28]], tbl_29[ids[:, 29]], tbl_30[ids[:, 30]], tbl_31[ids[:, 31]]], axis=1)
    z = _L0_rec_ref(e, L0_rec_kernels)
    z = z.reshape(z.shape[0], -1)
    h = jnp.concatenate([z, dense_ctx], axis=1)
    h = jnp.maximum(h @ W_top1 + b_top1, 0.0)
    h = jnp.maximum(h @ W_top2 + b_top2, 0.0)
    y = h @ W_top3
    return y

_drawn_inputs = setup_inputs


def setup_inputs(seed=0):
    import zlib

    import numpy as np

    out = dict(_drawn_inputs(seed))
    spreads = {'b_top1': (0.0, 0.1), 'b_top2': (0.0, 0.1)}
    factors = {'L0_rec_kernels': 64.0}
    for name, (base, spread) in spreads.items():
        noise = np.random.default_rng([zlib.crc32(name.encode()), seed]).standard_normal(out[name].shape)
        drawn = base * np.exp(spread * noise) if base else spread * noise
        out[name] = jnp.asarray(drawn.astype(out[name].dtype))
    for name, factor in factors.items():
        out[name] = (out[name] * factor).astype(out[name].dtype)
    return out
```

```python
from contextlib import ExitStack

import concourse.bass as bass
from concourse import mybir

SAMPLES, FEATURES, DIM = 1024, 32, 64
PAIRS = FEATURES * (FEATURES - 1) // 2
DENSE = 16
HIN, H1, H2 = FEATURES + PAIRS + DENSE, 512, 256
ROWS = 128
TILES = SAMPLES // ROWS
GF = 4
GROUPS = FEATURES // GF
GCOLS = GF * DIM
BANK = 512
BANK_PAIRS = BANK // DIM
UNIT_PAIRS = 16
UNIT_COLS = UNIT_PAIRS * DIM
Y_SLOTS = 3
T_SLOTS = 3
XT_SLOTS = 4
XT_AHEAD = 3
BLOCKS = 2
CHUNK_PAIRS = 16
CHUNK_COLS = CHUNK_PAIRS * DIM
CHUNKS = PAIRS // CHUNK_PAIRS
K_SLOTS = 3
KB = -(-HIN // 128)
KLAST = HIN - (KB - 1) * 128
ACT_SHARE = 0.33
EXTRAS = 5


def first_pair(i):
    return i * (FEATURES - 1) - i * (i - 1) // 2


def plan_units():
    steps = []
    for r in range(GROUPS):
        g = GROUPS - 1 - r
        rows = [i for i in range(GF * g + GF - 1, GF * g - 1, -1) if i < FEATURES - 1]
        units, small = [], []

        def close():
            if small:
                p0 = first_pair(small[-1])
                units.append((p0, sum(FEATURES - 1 - i for i in small),
                              [(i, i + 1, FEATURES - 1 - i, first_pair(i) - p0) for i in reversed(small)]))
                small.clear()

        for i in rows:
            n = FEATURES - 1 - i
            if sum(FEATURES - 1 - k for k in small) + n > UNIT_PAIRS:
                close()
            if n <= UNIT_PAIRS:
                small.append(i)
            else:
                half = (n + 1) // 2
                units.append((first_pair(i), half, [(i, i + 1, half, 0)]))
                units.append((first_pair(i) + half, n - half, [(i, i + 1 + half, n - half, 0)]))
        close()
        steps.append(units)
    return steps


STEPS = plan_units()
UNITS = [(r, unit) for r, step in enumerate(STEPS) for unit in step]
UPT = len(UNITS)
assert UPT % Y_SLOTS == 0 and UPT % T_SLOTS == 0
FIRST_UNIT = [sum(len(s) for s in STEPS[:r]) for r in range(GROUPS)]
ACT_PAIRS = [round(unit[1] * ACT_SHARE) for _, unit in UNITS]
ACT_SUMS = [sum(1 for a in ACT_PAIRS[:u + 1] if a) for u in range(UPT)]
APT = ACT_SUMS[-1]
CHUNK_OF = [(PAIRS - 1 - unit[0]) // CHUNK_PAIRS for _, unit in UNITS]


def tower_kernel(nc, dense_ctx, ids, tables, W1, b1, W2, b2, W3, K, out):
    f32, f32r, i32 = mybir.dt.float32, mybir.dt.float32r, mybir.dt.int32
    ALU = mybir.AluOpType
    ACT = mybir.ActivationFunctionType
    X_AXIS = mybir.AxisListType.X

    ids_v = ids.rearrange("(t p) f -> t p f", p=ROWS)
    dense_v = dense_ctx.rearrange("(t p) c -> t p c", p=ROWS)
    out_v = out.rearrange("(m k p) o -> m p (k o)", k=2, p=ROWS)

    ctx = ExitStack()
    with ctx:
        def sb(name, shape, dt):
            return ctx.enter_context(nc.sbuf_tensor(name, shape, dt))

        def ps(name, cols):
            return ctx.enter_context(nc.psum_tensor(name, [128, cols], f32))

        def sem(name):
            return ctx.enter_context(nc.semaphore(name))

        k_split = sb("k_split", [128, PAIRS * DIM], f32r)
        x = sb("x", [128, 2, FEATURES * DIM], f32)
        x_hi = sb("x_hi", [128, BLOCKS, GF, 2, DIM], f32r)
        x_lo = sb("x_lo", [128, BLOCKS, GF, 2, DIM], f32r)
        xt_hi = sb("xt_hi", [128, XT_SLOTS, GF, ROWS], f32r)
        xt_lo = sb("xt_lo", [128, XT_SLOTS, GF, ROWS], f32r)
        prod = sb("prod", [128, T_SLOTS, UNIT_COLS], f32)
        h_in = sb("h_in", [128, 2, HIN], f32)
        scratch = sb("scratch", [128, K_SLOTS * CHUNK_COLS], f32)
        hin_t = scratch[:, 0:KB * 256].rearrange("p (k b) -> p k b", k=KB)
        h1_t = scratch[:, KB * 256:KB * 256 + 4 * 256].rearrange("p (k b) -> p k b", k=4)
        h2_t = scratch[:, KB * 256 + 4 * 256:KB * 256 + 6 * 256].rearrange("p (k b) -> p k b", k=2)
        w1 = sb("w1", [128, KB, H1], f32)
        w2 = sb("w2", [128, H1 // 128, H2], f32)
        w3 = sb("w3", [128, H2 // 128], f32)
        bias1 = sb("bias1", [128, H1 // 128], f32)
        bias2 = sb("bias2", [128, H2 // 128], f32)
        ids_sb = sb("ids_sb", [128, 2, FEATURES], i32)
        ident = sb("ident", [128, 128], f32)
        ident_r = sb("ident_r", [128, 128], f32r)
        y_out = sb("y_out", [128, 2], f32)

        y = [ps(f"y{n}", UNIT_COLS) for n in range(Y_SLOTS)]
        aux_a, aux_b = ps("aux_a", BANK), ps("aux_b", BANK)

        ident_made = sem("ident_made")
        ident_ready = sem("ident_ready")
        k_in = [sem(f"k_in{n}") for n in range(K_SLOTS)]
        k_hi_done = sem("k_hi_done")
        k_ready = sem("k_ready")
        weights_in = sem("weights_in")
        ids_in = [sem(f"ids_in{n}") for n in range(2)]
        gathered = [[sem(f"gathered{k}_{r}") for r in range(GROUPS)] for k in range(2)]
        x_hi_done = sem("x_hi_done")
        x_lo_done = sem("x_lo_done")
        xt_filled = sem("xt_filled")
        xt_ready = sem("xt_ready")
        y_ready = sem("y_ready")
        prod_done = sem("prod_done")
        dve_summed = sem("dve_summed")
        act_summed = sem("act_summed")
        z_done = sem("z_done")
        dense_in = [sem(f"dense_in{n}") for n in range(2)]
        mlp_filled = sem("mlp_filled")
        mlp_drained = sem("mlp_drained")
        out_done = sem("out_done")

        block = ctx.enter_context(nc.Block())

        def wait(eng, semaphore, value):
            if not isinstance(value, int) or value > 0:
                eng.wait_ge(semaphore, value)

        def turned_of(m, half):
            return m * EXTRAS + 1 + half

        def layer(m, n):
            return m * EXTRAS + 2 + n

        def twice(cols):
            return cols.rearrange("b (f k d) -> b f k d", f=GF, k=1).to_broadcast([128, GF, 2, DIM])

        def pairs_of_tiles(eng, body):
            body(0, True, False)
            with eng.Fori(1, TILES // 2 - 1) as m:
                body(m, False, False)
            body(TILES // 2 - 1, False, True)

        @block.sync
        def _(sp):
            for c in range(CHUNKS):
                if c >= K_SLOTS:
                    sp.wait_ge(k_ready, c - K_SLOTS + 1)
                p0 = PAIRS - (c + 1) * CHUNK_PAIRS
                src = K[p0:p0 + CHUNK_PAIRS].rearrange("p d e -> d p e")
                s = c % K_SLOTS
                for lane in (0, DIM):
                    dst = scratch[lane:lane + DIM, s * CHUNK_COLS:(s + 1) * CHUNK_COLS]
                    sp.dma_start(dst.rearrange("d (p e) -> d p e", e=DIM), src).then_inc(k_in[s], 16)
            full = (KB - 1) * 128
            sp.dma_start(w1[:, 0:KB - 1, :], W1[0:full].rearrange("(k p) n -> p k n", p=128)).then_inc(weights_in, 16)
            sp.dma_start(w1[0:KLAST, KB - 1, :], W1[full:HIN]).then_inc(weights_in, 16)
            sp.dma_start(w2[:, :, :], W2.rearrange("(k p) n -> p k n", p=128)).then_inc(weights_in, 16)
            sp.dma_start(w3[:, :], W3.rearrange("(k p) o -> p (k o)", p=128), allow_slow_non_contiguous=True).then_inc(weights_in, 16)
            sp.dma_start(bias1[:, :], b1.rearrange("(k p) -> p k", p=128), allow_slow_non_contiguous=True).then_inc(weights_in, 16)
            sp.dma_start(bias2[:, :], b2.rearrange("(k p) -> p k", p=128), allow_slow_non_contiguous=True).then_inc(weights_in, 16)

            def body(m, first, last):
                for k in range(2):
                    if not first:
                        sp.wait_ge(mlp_filled, turned_of(m - 1, k))
                    sp.dma_start(h_in[:, k, FEATURES + PAIRS:HIN], dense_v[2 * m + k]).then_inc(dense_in[k], 16)
                if not first:
                    store(m - 1)

            def store(m):
                sp.wait_ge(mlp_drained, layer(m, 3))
                sp.dma_start(out_v[m], y_out[:, :], allow_slow_non_contiguous=True).then_inc(out_done, 16)

            pairs_of_tiles(sp, body)
            store(TILES // 2 - 1)
            sp.wait_ge(out_done, 16 * (TILES // 2))

        @block.gpsimd
        def _(pool):
            nc.gpsimd.memset(ident[:, :], 0.0).then_inc(ident_made, 1)
            pool.wait_ge(ident_made, 1)
            nc.gpsimd.affine_select(out=ident[:, :], in_=ident[:, :], compare_op=ALU.not_equal, fill=1.0,
                                    base=0, pattern=[[-1, 128]], channel_multiplier=1).then_inc(ident_made, 1)

            def load_ids(t, k):
                pool.dma_start(ids_sb[:, k, :], ids_v[t]).then_inc(ids_in[k], 16)

            def gather(k, r):
                g = GROUPS - 1 - r
                for f in range(GF * g, GF * g + GF):
                    nc.gpsimd.indirect_dma_start(
                        x[:, k, f * DIM:(f + 1) * DIM], None, tables[f],
                        bass.IndirectOffsetOnAxis(ap=ids_sb[:, k, f:f + 1], axis=0)).then_inc(gathered[k][r], 16)

            def low_part(m, k, r):
                q = (2 * m + k) * GROUPS + r
                g = GROUPS - 1 - r
                wait(pool, gathered[k][r], (m + 1) * 16 * GF)
                wait(pool, x_hi_done, q + 1)
                wait(pool, xt_filled, q + 1 - BLOCKS)
                nc.gpsimd.tensor_tensor(x_lo[:, r % BLOCKS], twice(x[:, k, g * GCOLS:(g + 1) * GCOLS]),
                                        x_hi[:, r % BLOCKS].bitcast(f32), ALU.subtract).then_inc(x_lo_done, 1)

            def next_tile(m, k, m2, k2, more):
                if more:
                    load_ids(2 * m + k + 2, k)
                wait(pool, ids_in[k2], (m2 + 1) * 16)
                before = 2 * m2 + k2 - 1
                wait(pool, prod_done, (before) * UPT)
                wait(pool, z_done, before)
                pool.nop(nofuse=True)
                for r in range(GROUPS // 2):
                    gather(k2, r)
                low_part(m2, k2, 0)
                gather(k2, 4)
                low_part(m2, k2, 1)
                gather(k2, 5)
                low_part(m2, k2, 2)
                gather(k2, 6)
                gather(k2, 7)
                low_part(m2, k2, 3)
                for r in range(4, GROUPS):
                    low_part(m2, k2, r)

            load_ids(0, 0)
            load_ids(1, 1)
            pool.wait_ge(ids_in[0], 16)
            for r in range(GROUPS + 1):
                if r < GROUPS:
                    gather(0, r)
                if r:
                    low_part(0, 0, r - 1)

            def body(m, first, last):
                next_tile(m, 0, m, 1, not last)
                if not last:
                    next_tile(m, 1, m + 1, 0, True)

            pairs_of_tiles(pool, body)

        @block.tensor
        def _(pe):
            def transpose_x(m, k, r, behind_mlp):
                q = (2 * m + k) * GROUPS + r
                wait(pe, x_lo_done, q + 1)
                wait(pe, xt_ready, q)
                if behind_mlp is not None:
                    pe.wait_ge(mlp_drained, behind_mlp)
                for part, bank in ((x_hi, aux_a), (x_lo, aux_b)):
                    for f in range(GF):
                        rows = part[:, r % BLOCKS, f].rearrange("b k d -> b (k d)")
                        last = nc.tensor.matmul(bank[:, f * ROWS:(f + 1) * ROWS], rows, ident_r[:, :],
                                                start=True, stop=True)
                last.then_inc(xt_filled, 1)

            def units(m, k, r, first):
                t = 2 * m + k
                q = t * GROUPS + r
                wait(pe, xt_ready, q + 1)
                for n, (p0, pairs, segments) in enumerate(STEPS[r]):
                    u = FIRST_UNIT[r] + n
                    if first and k == 0:
                        pe.wait_ge(k_ready, CHUNK_OF[u] + 1)
                    wait(pe, prod_done, t * UPT + u + 1 - Y_SLOTS)
                    dst = y[u % Y_SLOTS]
                    for i, _, count, place in segments:
                        cuts = [place] + [c for c in (BANK_PAIRS,) if place < c < place + count] + [place + count]
                        for part in (xt_hi, xt_lo):
                            for a, b in zip(cuts, cuts[1:]):
                                last = nc.tensor.matmul(
                                    dst[:, a * DIM:b * DIM], part[:, r % XT_SLOTS, i % GF, :],
                                    k_split[:, (p0 + a) * DIM:(p0 + b) * DIM],
                                    start=part is xt_hi, stop=part is xt_lo)
                    last.then_inc(y_ready, 1)

            def transpose_h(m, k):
                t = 2 * m + k
                wait(pe, dve_summed, (t + 1) * UPT)
                wait(pe, act_summed, (t + 1) * APT)
                wait(pe, z_done, t + 1)
                wait(pe, dense_in[k], (m + 1) * 16)
                for b in range(KB - 1):
                    nc.tensor.transpose(aux_a[:, b * ROWS:(b + 1) * ROWS], h_in[:, k, b * 128:(b + 1) * 128], ident[:, :])
                nc.tensor.transpose(aux_b[0:KLAST, 0:ROWS], h_in[:, k, (KB - 1) * 128:HIN], ident[:, :])\
                    .then_inc(mlp_filled, 1)

            def layer1(m):
                pe.wait_ge(mlp_drained, turned_of(m, 1))
                for n in range(H1 // 128):
                    dst = (aux_a, aux_b)[n // 2][:, n % 2 * 256:n % 2 * 256 + 256]
                    for b in range(KB):
                        rows = 128 if b < KB - 1 else KLAST
                        last = nc.tensor.matmul(dst, w1[0:rows, b, n * 128:(n + 1) * 128], hin_t[0:rows, b, :],
                                                start=b == 0, stop=b == KB - 1)
                last.then_inc(mlp_filled, 1)

            def layer2(m):
                pe.wait_ge(mlp_drained, layer(m, 1))
                for n in range(H2 // 128):
                    for b in range(H1 // 128):
                        last = nc.tensor.matmul(aux_a[:, n * 256:(n + 1) * 256], w2[:, b, n * 128:(n + 1) * 128],
                                                h1_t[:, b, :], start=b == 0, stop=b == H1 // 128 - 1)
                last.then_inc(mlp_filled, 1)

            def layer3(m):
                pe.wait_ge(mlp_drained, layer(m, 2))
                for k in range(2):
                    for b in range(H2 // 128):
                        last = nc.tensor.matmul(aux_a[:, k:k + 1], h2_t[:, b, k * ROWS:(k + 1) * ROWS],
                                                w3[:, b:b + 1], start=b == 0, stop=b == H2 // 128 - 1)
                last.then_inc(mlp_filled, 1)

            def body(m, first, last):
                behind = None
                for s in range(2 * GROUPS):
                    k, r = divmod(s, GROUPS)
                    units(m, k, r, first)
                    a = s + XT_AHEAD
                    if a < 2 * GROUPS:
                        transpose_x(m, a // GROUPS, a % GROUPS, behind)
                        behind = None
                    elif not last:
                        transpose_x(m + 1, 0, a % GROUPS, behind)
                        behind = None
                    now = (2 * m + (s + XT_AHEAD) // GROUPS) * GROUPS + (s + XT_AHEAD) % GROUPS + 1
                    if k == 0 and r >= 4 and not first:
                        wait(pe, xt_ready, now)
                        if r == 4:
                            transpose_h(m - 1, 1)
                            behind = turned_of(m - 1, 1)
                        else:
                            (layer1, layer2, layer3)[r - 5](m - 1)
                            behind = layer(m - 1, r - 4)
                    if k == 1 and r == 4:
                        wait(pe, xt_ready, now)
                        transpose_h(m, 0)
                        behind = turned_of(m, 0)

            pe.wait_ge(ident_ready, 1)
            for r in range(XT_AHEAD):
                transpose_x(0, 0, r, None)
            pe.wait_ge(ident_made, 2)

            body(0, True, False)
            pe.wait_ge(weights_in, 6 * 16)
            with pe.Fori(1, TILES // 2 - 1) as m:
                body(m, False, False)
            body(TILES // 2 - 1, False, True)
            m = TILES // 2 - 1
            transpose_h(m, 1)
            layer1(m)
            layer2(m)
            layer3(m)

        @block.vector
        def _(dve):
            dve.wait_ge(ident_made, 2)
            nc.vector.tensor_copy(ident_r[:, :], ident[:, :]).then_inc(ident_ready, 1)
            split = [0]

            def split_k(upto):
                while split[0] <= min(upto, CHUNKS - 1):
                    c = split[0]
                    split[0] += 1
                    p0 = PAIRS - (c + 1) * CHUNK_PAIRS
                    cols = k_split[DIM:128, p0 * DIM:p0 * DIM + CHUNK_COLS]
                    s = c % K_SLOTS
                    dve.wait_ge(k_hi_done, c + 1)
                    nc.vector.tensor_tensor(cols, scratch[DIM:128, s * CHUNK_COLS:(s + 1) * CHUNK_COLS],
                                            cols.bitcast(f32), ALU.subtract).then_inc(k_ready, 1)

            def sum_unit(t, k, u):
                p0, pairs, _ = UNITS[u][1]
                mine = pairs - ACT_PAIRS[u]
                dve.wait_ge(prod_done, t * UPT + u + 1)
                nc.vector.tensor_reduce(
                    h_in[:, k, FEATURES + p0:FEATURES + p0 + mine],
                    prod[:, u % T_SLOTS, 0:mine * DIM].rearrange("b (p e) -> b p e", e=DIM),
                    X_AXIS, ALU.add).then_inc(dve_summed, 1)

            def body(m, first, last):
                for k in range(2):
                    t = 2 * m + k
                    if not first:
                        dve.wait_ge(mlp_filled, turned_of(m - 1, k))
                    for u, (r, (p0, pairs, segments)) in enumerate(UNITS):
                        if first and k == 0:
                            split_k(CHUNK_OF[min(u + 3, UPT - 1)])
                        if u == FIRST_UNIT[r]:
                            dve.wait_ge(gathered[k][r], (m + 1) * 16 * GF)
                        dve.wait_ge(y_ready, t * UPT + u + 1)
                        before = u - T_SLOTS
                        wait(dve, act_summed, t * APT + ACT_SUMS[before] if before >= 0
                             else (t - 1) * APT + ACT_SUMS[before + UPT])
                        wait(dve, dve_summed, t * UPT + before + 1)
                        for n, (i, j, count, place) in enumerate(segments):
                            cols = slice(place * DIM, (place + count) * DIM)
                            done = nc.vector.tensor_tensor(prod[:, u % T_SLOTS, cols], y[u % Y_SLOTS][:, cols],
                                                           x[:, k, j * DIM:(j + count) * DIM], ALU.mult)
                        done.then_inc(prod_done, 1)
                        if u:
                            sum_unit(t, k, u - 1)
                    nc.vector.tensor_reduce(h_in[:, k, 0:FEATURES], x[:, k, :].rearrange("b (f e) -> b f e", e=DIM),
                                            X_AXIS, ALU.add).then_inc(z_done, 1)
                    sum_unit(t, k, UPT - 1)

            pairs_of_tiles(dve, body)

        @block.scalar
        def _(act):
            split = [0]

            def split_k(upto):
                while split[0] <= min(upto, CHUNKS - 1):
                    c = split[0]
                    split[0] += 1
                    p0 = PAIRS - (c + 1) * CHUNK_PAIRS
                    s = c % K_SLOTS
                    act.wait_ge(k_in[s], (c // K_SLOTS + 1) * 32)
                    nc.scalar.activation(k_split[:, p0 * DIM:p0 * DIM + CHUNK_COLS],
                                         scratch[:, s * CHUNK_COLS:(s + 1) * CHUNK_COLS], ACT.Copy)\
                        .then_inc(k_hi_done, 1)

            def high_part(m, k, r):
                q = (2 * m + k) * GROUPS + r
                g = GROUPS - 1 - r
                wait(act, gathered[k][r], (m + 1) * 16 * GF)
                wait(act, xt_filled, q + 1 - BLOCKS)
                wait(act, x_lo_done, q + 1 - BLOCKS)
                nc.scalar.activation(x_hi[:, r % BLOCKS], twice(x[:, k, g * GCOLS:(g + 1) * GCOLS]), ACT.Copy)\
                    .then_inc(x_hi_done, 1)

            def keep_x(m, k, r, first):
                q = (2 * m + k) * GROUPS + r
                wait(act, xt_filled, q + 1)
                nc.scalar.activation(xt_hi[:, r % XT_SLOTS, :, :].rearrange("p f b -> p (f b)"), aux_a[:, :], ACT.Copy)
                nc.scalar.activation(xt_lo[:, r % XT_SLOTS, :, :].rearrange("p f b -> p (f b)"), aux_b[:, :], ACT.Copy)\
                    .then_inc(xt_ready, 1)

            def sum_units(m, k, r, first):
                t = 2 * m + k
                for n, (p0, pairs, _) in enumerate(STEPS[r]):
                    u = FIRST_UNIT[r] + n
                    if first and k == 0:
                        split_k(CHUNK_OF[min(u + 5, UPT - 1)])
                    if not ACT_PAIRS[u]:
                        continue
                    act.wait_ge(prod_done, t * UPT + u + 1)
                    for p in range(pairs - ACT_PAIRS[u], pairs):
                        cols = prod[:, u % T_SLOTS, p * DIM:(p + 1) * DIM]
                        done = nc.scalar.activation(cols, cols, ACT.Copy,
                                                    accum_out=h_in[:, k, FEATURES + p0 + p:FEATURES + p0 + p + 1])
                    done.then_inc(act_summed, 1)

            def keep_h(m, k):
                act.wait_ge(mlp_filled, turned_of(m, k))
                nc.scalar.activation(hin_t[:, 0:KB - 1, k * ROWS:(k + 1) * ROWS],
                                     aux_a[:, :].rearrange("p (b c) -> p b c", b=KB - 1), ACT.Copy)
                nc.scalar.activation(hin_t[0:KLAST, KB - 1, k * ROWS:(k + 1) * ROWS], aux_b[0:KLAST, 0:ROWS], ACT.Copy)\
                    .then_inc(mlp_drained, 1)

            def relu1(m):
                act.wait_ge(mlp_filled, layer(m, 1))
                for n in range(H1 // 128):
                    src = (aux_a, aux_b)[n // 2][:, n % 2 * 256:n % 2 * 256 + 256]
                    done = nc.scalar.activation(h1_t[:, n, :], src, ACT.Relu, bias=bias1[:, n:n + 1])
                done.then_inc(mlp_drained, 1)

            def relu2(m):
                act.wait_ge(mlp_filled, layer(m, 2))
                for n in range(H2 // 128):
                    done = nc.scalar.activation(h2_t[:, n, :], aux_a[:, n * 256:(n + 1) * 256], ACT.Relu,
                                                bias=bias2[:, n:n + 1])
                done.then_inc(mlp_drained, 1)

            def keep_y(m):
                act.wait_ge(mlp_filled, layer(m, 3))
                wait(act, out_done, m * 16)
                nc.scalar.activation(y_out[:, :], aux_a[:, 0:2], ACT.Copy).then_inc(mlp_drained, 1)

            def body(m, first, last):
                for s in range(2 * GROUPS):
                    k, r = divmod(s, GROUPS)
                    a = s + XT_AHEAD + 1
                    if a < 2 * GROUPS:
                        high_part(m, a // GROUPS, a % GROUPS)
                    elif not last:
                        high_part(m + 1, 0, a % GROUPS)
                    if r == 0 and not first:
                        act.wait_ge(mlp_filled, turned_of(m - 1, k))
                    sum_units(m, k, r, first)
                    a = s + XT_AHEAD
                    if a < 2 * GROUPS:
                        keep_x(m, a // GROUPS, a % GROUPS, first)
                    elif not last:
                        keep_x(m + 1, 0, a % GROUPS, first)
                    if k == 0 and r >= 4 and not first:
                        if r == 4:
                            keep_h(m - 1, 1)
                        else:
                            (relu1, relu2, keep_y)[r - 5](m - 1)
                    if k == 1 and r == 4:
                        keep_h(m, 0)

            high_part(0, 0, 0)
            high_part(0, 0, 1)
            split_k(CHUNK_OF[2])
            keep_x(0, 0, 0, True)
            high_part(0, 0, 2)
            keep_x(0, 0, 1, True)
            high_part(0, 0, 3)
            keep_x(0, 0, 2, True)
            body(0, True, False)
            act.wait_ge(weights_in, 6 * 16)
            with act.Fori(1, TILES // 2 - 1) as m:
                body(m, False, False)
            body(TILES // 2 - 1, False, True)
            m = TILES // 2 - 1
            keep_h(m, 1)
            relu1(m)
            relu2(m)
            keep_y(m)


_INS = ["dense_ctx", "ids"] + [f"tbl_{f}" for f in range(32)] + ["W_top1", "b_top1", "W_top2", "b_top2", "W_top3",
                                                                "L0_rec_kernels"]
_OUT = ((1024, 1), "float32")


def kernel(**inputs):
    import numpy as _np
    import concourse.bacc as _bacc
    from concourse import mybir as _mybir
    from concourse.bass_utils import run_bass_kernel_spmd as _run

    nc = _bacc.Bacc("TRN2", target_bir_lowering=False, num_devices=1)
    arrays, args = {}, {}
    for name in _INS:
        a = _np.ascontiguousarray(inputs[name])
        arrays[f"in_{name}_dram"] = a
        args[name] = nc.dram_tensor(f"in_{name}_dram", a.shape, _mybir.dt.from_np(a.dtype), kind="ExternalInput").ap()
    out = nc.dram_tensor("out_0_dram", _OUT[0], _mybir.dt.from_np(_np.dtype(_OUT[1])), kind="ExternalOutput").ap()
    tower_kernel(nc, args["dense_ctx"], args["ids"], [args[f"tbl_{f}"] for f in range(32)], args["W_top1"],
                 args["b_top1"], args["W_top2"], args["b_top2"], args["W_top3"], args["L0_rec_kernels"], out)
    r = _run(nc, [arrays], core_ids=[0])
    return r.results[0]["out_0_dram"]
```

```python
from contextlib import ExitStack

import concourse.bass as bass
from concourse import mybir

SAMPLES, FEATURES, DIM = 1024, 32, 64
PAIRS = FEATURES * (FEATURES - 1) // 2
DENSE = 16
HIN, H1, H2 = FEATURES + PAIRS + DENSE, 512, 256
ROWS = 128
TILES = SAMPLES // ROWS
GF = 4
GROUPS = FEATURES // GF
GCOLS = GF * DIM
BANK = 512
BANK_PAIRS = BANK // DIM
UNIT_PAIRS = 16
UNIT_COLS = UNIT_PAIRS * DIM
Y_SLOTS = 3
T_SLOTS = 3
XT_SLOTS = 4
BLOCKS = 2
CHUNK_PAIRS = 16
CHUNK_COLS = CHUNK_PAIRS * DIM
CHUNKS = PAIRS // CHUNK_PAIRS
K_SLOTS = 3
K_AHEAD = 8
KB = -(-HIN // 128)
KLAST = HIN - (KB - 1) * 128
ACT_SHARE = 0.33
L1_PIECES, L2_PIECES = H1 // 128, H2 // 128
MLP_USES = 2 + L1_PIECES + L2_PIECES + 1


def first_pair(i):
    return i * (FEATURES - 1) - i * (i - 1) // 2


def plan_units():
    steps = []
    for r in range(GROUPS):
        g = GROUPS - 1 - r
        rows = [i for i in range(GF * g + GF - 1, GF * g - 1, -1) if i < FEATURES - 1]
        units, small = [], []

        def close():
            if small:
                p0 = first_pair(small[-1])
                units.append((p0, sum(FEATURES - 1 - i for i in small),
                              [(i, i + 1, FEATURES - 1 - i, first_pair(i) - p0) for i in reversed(small)]))
                small.clear()

        for i in rows:
            n = FEATURES - 1 - i
            if sum(FEATURES - 1 - k for k in small) + n > UNIT_PAIRS:
                close()
            if n <= UNIT_PAIRS:
                small.append(i)
            else:
                half = (n + 1) // 2
                units.append((first_pair(i), half, [(i, i + 1, half, 0)]))
                units.append((first_pair(i) + half, n - half, [(i, i + 1 + half, n - half, 0)]))
        close()
        steps.append(units)
    return steps


STEPS = plan_units()
UNITS = [(r, unit) for r, step in enumerate(STEPS) for unit in step]
UPT = len(UNITS)
assert UPT % Y_SLOTS == 0 and UPT % T_SLOTS == 0
FIRST_UNIT = [sum(len(s) for s in STEPS[:r]) for r in range(GROUPS)]
ACT_PAIRS = [round(unit[1] * ACT_SHARE) for _, unit in UNITS]
ACT_SUMS = [sum(1 for a in ACT_PAIRS[:u + 1] if a) for u in range(UPT)]
APT = ACT_SUMS[-1]

TURN_AT = [29 - UPT, 33 - UPT, 37 - UPT, 1, 4, 8, 13, 20]
HIGH_AT = [max(TURN_AT[r] - 6, (TURN_AT + [p - UPT for p in TURN_AT])[r - 2] - 1) for r in range(GROUPS)]
HIGH_AT[0], HIGH_AT[1] = TURN_AT[0] - 6, TURN_AT[1] - 6
MLP_AT = [[(10, ("h", 1)), (15, ("l1", 0)), (17, ("l1", 1)), (22, ("l1", 2)), (24, ("l1", 3)), (26, ("l2", 0)),
           (31, ("l2", 1)), (35, ("l3", 0))], [(10, ("h", 0))]]
CHUNK_OF = [(PAIRS - 1 - unit[0]) // CHUNK_PAIRS for _, unit in UNITS]


def plan_tile(k):
    aux = sorted([(p % UPT, ("x", int(p < 0), r)) for r, p in enumerate(TURN_AT)] + MLP_AT[k])
    high = sorted(((p % UPT, (int(p < 0), r)) for r, p in enumerate(HIGH_AT)), key=lambda e: (e[0], -e[1][0], e[1][1]))
    return aux, high


def tower_kernel(nc, dense_ctx, ids, tables, W1, b1, W2, b2, W3, K, out):
    f32, f32r, i32 = mybir.dt.float32, mybir.dt.float32r, mybir.dt.int32
    ALU = mybir.AluOpType
    ACT = mybir.ActivationFunctionType
    X_AXIS = mybir.AxisListType.X

    ids_v = ids.rearrange("(t p) f -> t p f", p=ROWS)
    dense_v = dense_ctx.rearrange("(t p) c -> t p c", p=ROWS)
    out_v = out.rearrange("(m k p) o -> m p (k o)", k=2, p=ROWS)

    ctx = ExitStack()
    with ctx:
        def sb(name, shape, dt):
            return ctx.enter_context(nc.sbuf_tensor(name, shape, dt))

        def ps(name, cols):
            return ctx.enter_context(nc.psum_tensor(name, [128, cols], f32))

        def sem(name):
            return ctx.enter_context(nc.semaphore(name))

        k_split = sb("k_split", [128, PAIRS * DIM], f32r)
        x = sb("x", [128, 2, FEATURES * DIM], f32)
        x_hi = sb("x_hi", [128, BLOCKS, GF, 2, DIM], f32r)
        x_lo = sb("x_lo", [128, BLOCKS, GF, 2, DIM], f32r)
        xt_hi = sb("xt_hi", [128, XT_SLOTS, GF, ROWS], f32r)
        xt_lo = sb("xt_lo", [128, XT_SLOTS, GF, ROWS], f32r)
        prod = sb("prod", [128, T_SLOTS, UNIT_COLS], f32)
        h_in = sb("h_in", [128, 2, HIN], f32)
        scratch = sb("scratch", [128, K_SLOTS * CHUNK_COLS], f32)
        hin_t = scratch[:, 0:KB * 256].rearrange("p (k b) -> p k b", k=KB)
        h1_t = scratch[:, KB * 256:KB * 256 + 4 * 256].rearrange("p (k b) -> p k b", k=4)
        h2_t = scratch[:, KB * 256 + 4 * 256:KB * 256 + 6 * 256].rearrange("p (k b) -> p k b", k=2)
        w1 = sb("w1", [128, KB, H1], f32)
        w2 = sb("w2", [128, H1 // 128, H2], f32)
        w3 = sb("w3", [128, H2 // 128], f32)
        bias1 = sb("bias1", [128, H1 // 128], f32)
        bias2 = sb("bias2", [128, H2 // 128], f32)
        ids_sb = sb("ids_sb", [128, 2, FEATURES], i32)
        ident = sb("ident", [128, 128], f32)
        ident_r = sb("ident_r", [128, 128], f32r)
        y_out = sb("y_out", [128, 2], f32)

        y = [ps(f"y{n}", UNIT_COLS) for n in range(Y_SLOTS)]
        aux_a, aux_b = ps("aux_a", BANK), ps("aux_b", BANK)

        ident_made = sem("ident_made")
        ident_ready = sem("ident_ready")
        k_in = [sem(f"k_in{n}") for n in range(K_SLOTS)]
        k_hi_done = sem("k_hi_done")
        k_ready = sem("k_ready")
        weights_in = sem("weights_in")
        ids_in = [sem(f"ids_in{n}") for n in range(2)]
        gathered = [[sem(f"gathered{k}_{r}") for r in range(GROUPS)] for k in range(2)]
        x_hi_done = sem("x_hi_done")
        x_lo_done = sem("x_lo_done")
        xt_filled = sem("xt_filled")
        xt_ready = sem("xt_ready")
        y_ready = sem("y_ready")
        prod_done = sem("prod_done")
        dve_summed = sem("dve_summed")
        act_summed = sem("act_summed")
        z_done = sem("z_done")
        dense_in = [sem(f"dense_in{n}") for n in range(2)]
        mlp_filled = sem("mlp_filled")
        mlp_drained = sem("mlp_drained")
        out_done = sem("out_done")

        block = ctx.enter_context(nc.Block())

        def wait(eng, semaphore, value):
            if not isinstance(value, int) or value > 0:
                eng.wait_ge(semaphore, value)

        def turned_of(m, half):
            return m * MLP_USES + 1 + half

        def part_of(m, part):
            kind, n = part
            return m * MLP_USES + 1 + n + {"h": 0, "l1": 2, "l2": 2 + L1_PIECES, "l3": 2 + L1_PIECES + L2_PIECES}[kind]

        def twice(cols):
            return cols.rearrange("b (f k d) -> b f k d", f=GF, k=1).to_broadcast([128, GF, 2, DIM])

        def pairs_of_tiles(eng, body):
            body(0, True, False)
            with eng.Fori(1, TILES // 2 - 1) as m:
                body(m, False, False)
            body(TILES // 2 - 1, False, True)

        @block.sync
        def _(sp):
            for c in range(CHUNKS):
                if c >= K_SLOTS:
                    sp.wait_ge(k_ready, c - K_SLOTS + 1)
                p0 = PAIRS - (c + 1) * CHUNK_PAIRS
                src = K[p0:p0 + CHUNK_PAIRS].rearrange("p d e -> d p e")
                s = c % K_SLOTS
                dst = scratch[0:DIM, s * CHUNK_COLS:(s + 1) * CHUNK_COLS]
                sp.dma_start(dst.rearrange("d (p e) -> d p e", e=DIM), src).then_inc(k_in[s], 16)
            full = (KB - 1) * 128
            sp.dma_start(w1[:, 0:KB - 1, :], W1[0:full].rearrange("(k p) n -> p k n", p=128)).then_inc(weights_in, 16)
            sp.dma_start(w1[0:KLAST, KB - 1, :], W1[full:HIN]).then_inc(weights_in, 16)
            sp.dma_start(w2[:, :, :], W2.rearrange("(k p) n -> p k n", p=128)).then_inc(weights_in, 16)
            sp.dma_start(w3[:, :], W3.rearrange("(k p) o -> p (k o)", p=128), allow_slow_non_contiguous=True).then_inc(weights_in, 16)
            sp.dma_start(bias1[:, :], b1.rearrange("(k p) -> p k", p=128), allow_slow_non_contiguous=True).then_inc(weights_in, 16)
            sp.dma_start(bias2[:, :], b2.rearrange("(k p) -> p k", p=128), allow_slow_non_contiguous=True).then_inc(weights_in, 16)

            def body(m, first, last):
                for k in range(2):
                    if not first:
                        sp.wait_ge(mlp_filled, turned_of(m - 1, k))
                    sp.dma_start(h_in[:, k, FEATURES + PAIRS:HIN], dense_v[2 * m + k]).then_inc(dense_in[k], 16)
                if not first:
                    store(m - 1)

            def store(m):
                sp.wait_ge(mlp_drained, part_of(m, ("l3", 0)))
                sp.dma_start(out_v[m], y_out[:, :], allow_slow_non_contiguous=True).then_inc(out_done, 16)

            pairs_of_tiles(sp, body)
            store(TILES // 2 - 1)
            sp.wait_ge(out_done, 16 * (TILES // 2))

        @block.gpsimd
        def _(pool):
            nc.gpsimd.memset(ident[:, :], 0.0).then_inc(ident_made, 1)
            pool.wait_ge(ident_made, 1)
            nc.gpsimd.affine_select(out=ident[:, :], in_=ident[:, :], compare_op=ALU.not_equal, fill=1.0,
                                    base=0, pattern=[[-1, 128]], channel_multiplier=1).then_inc(ident_made, 1)

            def load_ids(t, k):
                pool.dma_start(ids_sb[:, k, :], ids_v[t]).then_inc(ids_in[k], 16)

            def gather(k, r):
                g = GROUPS - 1 - r
                for f in range(GF * g, GF * g + GF):
                    nc.gpsimd.indirect_dma_start(
                        x[:, k, f * DIM:(f + 1) * DIM], None, tables[f],
                        bass.IndirectOffsetOnAxis(ap=ids_sb[:, k, f:f + 1], axis=0)).then_inc(gathered[k][r], 16)

            def low_part(m, k, r):
                q = (2 * m + k) * GROUPS + r
                g = GROUPS - 1 - r
                wait(pool, gathered[k][r], (m + 1) * 16 * GF)
                wait(pool, x_hi_done, q + 1)
                wait(pool, xt_filled, q + 1 - BLOCKS)
                nc.gpsimd.tensor_tensor(x_lo[:, r % BLOCKS], twice(x[:, k, g * GCOLS:(g + 1) * GCOLS]),
                                        x_hi[:, r % BLOCKS].bitcast(f32), ALU.subtract).then_inc(x_lo_done, 1)

            def x_free(m2, k2):
                wait(pool, ids_in[k2], (m2 + 1) * 16)
                before = 2 * m2 + k2 - 1
                wait(pool, prod_done, before * UPT)
                wait(pool, z_done, before)
                pool.nop(nofuse=True)

            def tile(m, k, m2, k2, more, first, last):
                if not first:
                    low_part(m, k, 3)
                    low_part(m, k, 4)
                if not last:
                    x_free(m2, k2)
                    gather(k2, 0)
                if not first:
                    low_part(m, k, 5)
                if not last:
                    gather(k2, 1)
                if not first:
                    low_part(m, k, 6)
                if not last:
                    gather(k2, 2)
                    gather(k2, 3)
                low_part(m, k, 7)
                if more:
                    load_ids(2 * m + k + 2, k)
                if not last:
                    gather(k2, 4)
                    gather(k2, 5)
                    gather(k2, 6)
                    low_part(m2, k2, 0)
                    gather(k2, 7)
                    low_part(m2, k2, 1)
                    low_part(m2, k2, 2)

            load_ids(0, 0)
            load_ids(1, 1)
            pool.wait_ge(ids_in[0], 16)
            for r in range(GROUPS):
                gather(0, r)
                if r:
                    low_part(0, 0, r - 1)

            def body(m, first, last):
                tile(m, 0, m, 1, not last, first, False)
                tile(m, 1, m + 1, 0, not last, False, last)

            pairs_of_tiles(pool, body)

        @block.tensor
        def _(pe):
            def transpose_x(m, k, r):
                q = (2 * m + k) * GROUPS + r
                wait(pe, x_lo_done, q + 1)
                for part, bank in ((x_hi, aux_a), (x_lo, aux_b)):
                    for f in range(GF):
                        rows = part[:, r % BLOCKS, f].rearrange("b k d -> b (k d)")
                        last = nc.tensor.matmul(bank[:, f * ROWS:(f + 1) * ROWS], rows, ident_r[:, :],
                                                start=True, stop=True)
                last.then_inc(xt_filled, 1)

            def make_y(m, k, u, first):
                t = 2 * m + k
                r, (p0, pairs, segments) = UNITS[u]
                if u == FIRST_UNIT[r]:
                    wait(pe, xt_ready, t * GROUPS + r + 1)
                if first and k == 0:
                    pe.wait_ge(k_ready, CHUNK_OF[u] + 1)
                wait(pe, prod_done, t * UPT + u + 1 - Y_SLOTS)
                dst = y[u % Y_SLOTS]
                for i, _, count, place in segments:
                    cuts = [place] + [c for c in (BANK_PAIRS,) if place < c < place + count] + [place + count]
                    for part in (xt_hi, xt_lo):
                        for a, b in zip(cuts, cuts[1:]):
                            last = nc.tensor.matmul(
                                dst[:, a * DIM:b * DIM], part[:, r % XT_SLOTS, i % GF, :],
                                k_split[:, (p0 + a) * DIM:(p0 + b) * DIM],
                                start=part is xt_hi, stop=part is xt_lo)
                last.then_inc(y_ready, 1)

            def transpose_h(m, k):
                t = 2 * m + k
                wait(pe, dve_summed, (t + 1) * UPT)
                wait(pe, act_summed, (t + 1) * APT)
                wait(pe, z_done, t + 1)
                wait(pe, dense_in[k], (m + 1) * 16)
                for b in range(KB - 1):
                    nc.tensor.transpose(aux_a[:, b * ROWS:(b + 1) * ROWS], h_in[:, k, b * 128:(b + 1) * 128], ident[:, :])
                nc.tensor.transpose(aux_b[0:KLAST, 0:ROWS], h_in[:, k, (KB - 1) * 128:HIN], ident[:, :])\
                    .then_inc(mlp_filled, 1)

            def layer1(m, n):
                if n == 0:
                    pe.wait_ge(mlp_drained, turned_of(m, 1))
                for b in range(KB):
                    rows = 128 if b < KB - 1 else KLAST
                    last = nc.tensor.matmul(aux_a[:, 0:256], w1[0:rows, b, n * 128:(n + 1) * 128],
                                            hin_t[0:rows, b, :], start=b == 0, stop=b == KB - 1)
                last.then_inc(mlp_filled, 1)

            def layer2(m, n):
                if n == 0:
                    pe.wait_ge(mlp_drained, part_of(m, ("l1", L1_PIECES - 1)))
                for b in range(H1 // 128):
                    last = nc.tensor.matmul(aux_a[:, 0:256], w2[:, b, n * 128:(n + 1) * 128],
                                            h1_t[:, b, :], start=b == 0, stop=b == H1 // 128 - 1)
                last.then_inc(mlp_filled, 1)

            def layer3(m, _):
                pe.wait_ge(mlp_drained, part_of(m, ("l2", L2_PIECES - 1)))
                for k in range(2):
                    for b in range(H2 // 128):
                        last = nc.tensor.matmul(aux_a[:, k:k + 1], h2_t[:, b, k * ROWS:(k + 1) * ROWS],
                                                w3[:, b:b + 1], start=b == 0, stop=b == H2 // 128 - 1)
                last.then_inc(mlp_filled, 1)

            mlp = {"h": transpose_h, "l1": layer1, "l2": layer2, "l3": layer3}

            def body(m, first, last):
                before = ("x", 0, 2)
                for k in range(2):
                    aux, _ = plan_tile(k)
                    for u in range(UPT + 1):
                        for _, part in [e for e in aux if e[0] == u]:
                            if part[0] == "x" and part[1] and last and k:
                                continue
                            if part[0] != "x" and first and k == 0:
                                continue
                            if before[0] == "x":
                                wait(pe, xt_ready, (2 * m + before[1]) * GROUPS + before[2] + 1)
                            else:
                                pe.wait_ge(mlp_drained, part_of(m - 1 + k, before))
                            if part[0] == "x":
                                ahead = k + part[1]
                                transpose_x(m + ahead // 2, ahead % 2, part[2])
                                before = ("x", ahead, part[2])
                            else:
                                mlp[part[0]](m - 1 + k, part[1])
                                before = part
                        if u < UPT:
                            make_y(m, k, u, first)

            pe.wait_ge(ident_ready, 1)
            for r in range(3):
                wait(pe, xt_ready, r)
                transpose_x(0, 0, r)
            pe.wait_ge(ident_made, 2)
            body(0, True, False)
            pe.wait_ge(weights_in, 6 * 16)
            with pe.Fori(1, TILES // 2 - 1) as m:
                body(m, False, False)
            m = TILES // 2 - 1
            body(m, False, True)
            before = None
            for part in [("h", 1)] + [part for _, part in MLP_AT[0][1:]]:
                if before:
                    pe.wait_ge(mlp_drained, part_of(m, before))
                mlp[part[0]](m, part[1])
                before = part

        @block.vector
        def _(dve):
            dve.wait_ge(ident_made, 2)
            nc.vector.tensor_copy(ident_r[:, :], ident[:, :]).then_inc(ident_ready, 1)
            split = [0]

            def split_k(upto):
                while split[0] <= min(upto, CHUNKS - 1):
                    c = split[0]
                    split[0] += 1
                    p0 = PAIRS - (c + 1) * CHUNK_PAIRS
                    cols = slice(p0 * DIM, p0 * DIM + CHUNK_COLS)
                    s = c % K_SLOTS
                    dve.wait_ge(k_hi_done, c + 1)
                    nc.vector.tensor_tensor(k_split[DIM:128, cols], scratch[0:DIM, s * CHUNK_COLS:(s + 1) * CHUNK_COLS],
                                            k_split[0:DIM, cols].bitcast(f32), ALU.subtract).then_inc(k_ready, 1)

            def sum_unit(t, k, u):
                p0, pairs, _ = UNITS[u][1]
                mine = pairs - ACT_PAIRS[u]
                dve.wait_ge(prod_done, t * UPT + u + 1)
                nc.vector.tensor_reduce(
                    h_in[:, k, FEATURES + p0:FEATURES + p0 + mine],
                    prod[:, u % T_SLOTS, 0:mine * DIM].rearrange("b (p e) -> b p e", e=DIM),
                    X_AXIS, ALU.add).then_inc(dve_summed, 1)

            def body(m, first, last):
                for k in range(2):
                    t = 2 * m + k
                    if not first:
                        dve.wait_ge(mlp_filled, turned_of(m - 1, k))
                    for u, (r, (p0, pairs, segments)) in enumerate(UNITS):
                        if first and k == 0:
                            split_k(CHUNK_OF[min(u + K_AHEAD, UPT - 1)])
                        if u == FIRST_UNIT[r]:
                            dve.wait_ge(gathered[k][r], (m + 1) * 16 * GF)
                        dve.wait_ge(y_ready, t * UPT + u + 1)
                        before = u - T_SLOTS
                        wait(dve, act_summed, t * APT + ACT_SUMS[before] if before >= 0
                             else (t - 1) * APT + ACT_SUMS[before + UPT])
                        wait(dve, dve_summed, t * UPT + before + 1)
                        for n, (i, j, count, place) in enumerate(segments):
                            cols = slice(place * DIM, (place + count) * DIM)
                            done = nc.vector.tensor_tensor(prod[:, u % T_SLOTS, cols], y[u % Y_SLOTS][:, cols],
                                                           x[:, k, j * DIM:(j + count) * DIM], ALU.mult)
                        done.then_inc(prod_done, 1)
                        if u:
                            sum_unit(t, k, u - 1)
                    nc.vector.tensor_reduce(h_in[:, k, 0:FEATURES], x[:, k, :].rearrange("b (f e) -> b f e", e=DIM),
                                            X_AXIS, ALU.add).then_inc(z_done, 1)
                    sum_unit(t, k, UPT - 1)

            pairs_of_tiles(dve, body)

        @block.scalar
        def _(act):
            split = [0]

            def split_k(upto):
                while split[0] <= min(upto, CHUNKS - 1):
                    c = split[0]
                    split[0] += 1
                    p0 = PAIRS - (c + 1) * CHUNK_PAIRS
                    s = c % K_SLOTS
                    act.wait_ge(k_in[s], (c // K_SLOTS + 1) * 16)
                    nc.scalar.activation(k_split[0:DIM, p0 * DIM:p0 * DIM + CHUNK_COLS],
                                         scratch[0:DIM, s * CHUNK_COLS:(s + 1) * CHUNK_COLS], ACT.Copy)\
                        .then_inc(k_hi_done, 1)

            def high_part(m, k, r):
                q = (2 * m + k) * GROUPS + r
                g = GROUPS - 1 - r
                wait(act, gathered[k][r], (m + 1) * 16 * GF)
                wait(act, xt_filled, q + 1 - BLOCKS)
                wait(act, x_lo_done, q + 1 - BLOCKS)
                nc.scalar.activation(x_hi[:, r % BLOCKS], twice(x[:, k, g * GCOLS:(g + 1) * GCOLS]), ACT.Copy)\
                    .then_inc(x_hi_done, 1)

            def keep_x(m, k, r):
                q = (2 * m + k) * GROUPS + r
                wait(act, xt_filled, q + 1)
                nc.scalar.activation(xt_hi[:, r % XT_SLOTS, :, :].rearrange("p f b -> p (f b)"), aux_a[:, :], ACT.Copy)
                nc.scalar.activation(xt_lo[:, r % XT_SLOTS, :, :].rearrange("p f b -> p (f b)"), aux_b[:, :], ACT.Copy)\
                    .then_inc(xt_ready, 1)

            def sum_unit(m, k, u, first):
                if first and k == 0:
                    split_k(CHUNK_OF[min(u + 2 + K_AHEAD, UPT - 1)])
                if not ACT_PAIRS[u]:
                    return
                p0, pairs, _ = UNITS[u][1]
                act.wait_ge(prod_done, (2 * m + k) * UPT + u + 1)
                for p in range(pairs - ACT_PAIRS[u], pairs):
                    cols = prod[:, u % T_SLOTS, p * DIM:(p + 1) * DIM]
                    done = nc.scalar.activation(cols, cols, ACT.Copy,
                                                accum_out=h_in[:, k, FEATURES + p0 + p:FEATURES + p0 + p + 1])
                done.then_inc(act_summed, 1)

            def keep_h(m, k):
                act.wait_ge(mlp_filled, turned_of(m, k))
                nc.scalar.activation(hin_t[:, 0:KB - 1, k * ROWS:(k + 1) * ROWS],
                                     aux_a[:, :].rearrange("p (b c) -> p b c", b=KB - 1), ACT.Copy)
                nc.scalar.activation(hin_t[0:KLAST, KB - 1, k * ROWS:(k + 1) * ROWS], aux_b[0:KLAST, 0:ROWS], ACT.Copy)\
                    .then_inc(mlp_drained, 1)

            def relu1(m, n):
                act.wait_ge(mlp_filled, part_of(m, ("l1", n)))
                nc.scalar.activation(h1_t[:, n, :], aux_a[:, 0:256], ACT.Relu, bias=bias1[:, n:n + 1])\
                    .then_inc(mlp_drained, 1)

            def relu2(m, n):
                act.wait_ge(mlp_filled, part_of(m, ("l2", n)))
                nc.scalar.activation(h2_t[:, n, :], aux_a[:, 0:256], ACT.Relu, bias=bias2[:, n:n + 1])\
                    .then_inc(mlp_drained, 1)

            def keep_y(m, _):
                act.wait_ge(mlp_filled, part_of(m, ("l3", 0)))
                wait(act, out_done, m * 16)
                nc.scalar.activation(y_out[:, :], aux_a[:, 0:2], ACT.Copy).then_inc(mlp_drained, 1)

            mlp = {"h": keep_h, "l1": relu1, "l2": relu2, "l3": keep_y}

            def body(m, first, last):
                for k in range(2):
                    aux, high = plan_tile(k)
                    for u in range(UPT):
                        for _, (ahead, r) in [e for e in high if e[0] == u]:
                            if ahead and last and k:
                                continue
                            high_part(m + (k + ahead) // 2, (k + ahead) % 2, r)
                        for _, part in [e for e in aux if e[0] == u + 1 or e[0] == 0 == u]:
                            if part[0] == "x":
                                if part[1] and last and k:
                                    continue
                                keep_x(m + (k + part[1]) // 2, (k + part[1]) % 2, part[2])
                            elif not (first and k == 0):
                                mlp[part[0]](m - 1 + k, part[1])
                        if u == 0 and not first:
                            act.wait_ge(mlp_filled, turned_of(m - 1, k))
                        sum_unit(m, k, u, first)

            split_k(2)
            high_part(0, 0, 0)
            split_k(4)
            high_part(0, 0, 1)
            keep_x(0, 0, 0)
            split_k(6)
            high_part(0, 0, 2)
            keep_x(0, 0, 1)
            high_part(0, 0, 3)
            keep_x(0, 0, 2)
            high_part(0, 0, 4)
            body(0, True, False)
            act.wait_ge(weights_in, 6 * 16)
            with act.Fori(1, TILES // 2 - 1) as m:
                body(m, False, False)
            m = TILES // 2 - 1
            body(m, False, True)
            for part in [("h", 1)] + [part for _, part in MLP_AT[0][1:]]:
                mlp[part[0]](m, part[1])


_INS = ["dense_ctx", "ids"] + [f"tbl_{f}" for f in range(32)] + ["W_top1", "b_top1", "W_top2", "b_top2", "W_top3",
                                                                "L0_rec_kernels"]
_OUT = ((1024, 1), "float32")


def kernel(**inputs):
    import numpy as _np
    import concourse.bacc as _bacc
    from concourse import mybir as _mybir
    from concourse.bass_utils import run_bass_kernel_spmd as _run

    nc = _bacc.Bacc("TRN2", target_bir_lowering=False, num_devices=1)
    arrays, args = {}, {}
    for name in _INS:
        a = _np.ascontiguousarray(inputs[name])
        arrays[f"in_{name}_dram"] = a
        args[name] = nc.dram_tensor(f"in_{name}_dram", a.shape, _mybir.dt.from_np(a.dtype), kind="ExternalInput").ap()
    out = nc.dram_tensor("out_0_dram", _OUT[0], _mybir.dt.from_np(_np.dtype(_OUT[1])), kind="ExternalOutput").ap()
    tower_kernel(nc, args["dense_ctx"], args["ids"], [args[f"tbl_{f}"] for f in range(32)], args["W_top1"],
                 args["b_top1"], args["W_top2"], args["b_top2"], args["W_top3"], args["L0_rec_kernels"], out)
    r = _run(nc, [arrays], core_ids=[0])
    return r.results[0]["out_0_dram"]
```

```python
from contextlib import ExitStack

import concourse.bass as bass
from concourse import mybir

SAMPLES, FEATURES, DIM = 1024, 32, 64
PAIRS = FEATURES * (FEATURES - 1) // 2
DENSE = 16
HIN, H1, H2 = FEATURES + PAIRS + DENSE, 512, 256
ROWS = 128
TILES = SAMPLES // ROWS
GF = 4
GROUPS = FEATURES // GF
GCOLS = GF * DIM
BANK = 512
BANK_PAIRS = BANK // DIM
UNIT_PAIRS = 16
UNIT_COLS = UNIT_PAIRS * DIM
Y_SLOTS = 3
T_SLOTS = 3
XT_SLOTS = 4
BLOCKS = 2
CHUNK_PAIRS = 16
CHUNK_COLS = CHUNK_PAIRS * DIM
CHUNKS = PAIRS // CHUNK_PAIRS
K_SLOTS = 3
K_AHEAD = 8
KB = -(-HIN // 128)
KLAST = HIN - (KB - 1) * 128
DVE_OP, DVE_PAIR = 65, 67
ACT_PAIR, ACT_COPY = 240, 500
ACT_BACKLOG = 400
FOLD_MIN_PAIRS = 11


def first_pair(i):
    return i * (FEATURES - 1) - i * (i - 1) // 2


def plan_units():
    steps = []
    for r in range(GROUPS):
        g = GROUPS - 1 - r
        rows = [i for i in range(GF * g + GF - 1, GF * g - 1, -1) if i < FEATURES - 1]
        units, small = [], []

        def close():
            if small:
                p0 = first_pair(small[-1])
                units.append((p0, sum(FEATURES - 1 - i for i in small),
                              [(i, i + 1, FEATURES - 1 - i, first_pair(i) - p0) for i in reversed(small)]))
                small.clear()

        for i in rows:
            n = FEATURES - 1 - i
            if sum(FEATURES - 1 - k for k in small) + n > UNIT_PAIRS:
                close()
            if n <= UNIT_PAIRS:
                small.append(i)
            else:
                half = (n + 1) // 2
                units.append((first_pair(i), half, [(i, i + 1, half, 0)]))
                units.append((first_pair(i) + half, n - half, [(i, i + 1 + half, n - half, 0)]))
        close()
        steps.append(units)
    return steps


STEPS = plan_units()
UNITS = [(r, unit) for r, step in enumerate(STEPS) for unit in step]
UPT = len(UNITS)
assert UPT % Y_SLOTS == 0 and UPT % T_SLOTS == 0
FIRST_UNIT = [sum(len(s) for s in STEPS[:r]) for r in range(GROUPS)]
FOLDED = [u for u in range(UPT) if u % 2 == 0 and UNITS[u][1][1] >= FOLD_MIN_PAIRS]
FPT = len(FOLDED)
FIRST_FOLDED = [u for u in FOLDED if u >= 14]
LAST_FOLDED = [u for u in range(8, UPT) if UNITS[u][1][1] >= 8]

TURN_AT = [(-18, -15), (-12, -9), (-7, -4), (0, 2), (5, 7), (10, 12), (15, 17), (19, 21)]
HIGH_AT = [max(TURN_AT[r][0] - 7, TURN_AT[r - 2][1] - 1 - (UPT if r < 2 else 0)) for r in range(GROUPS)]
LOW_AT = [p + 2 for p in HIGH_AT]
FIRST_TURN_AT = [(None, None), (1, 1), (2, 3), (4, 5), (7, 8), (10, 12), (14, 16), (18, 20)]
FIRST_HIGH_AT = [None, None, 0, 1, 3, 5, 8, 12]
FIRST_LOWS_AT = [None, None, 1, 2]
FIRST_LOWS = len(FIRST_LOWS_AT)
MLP_PLAN = [(("h1", 0), [4]), (("h1", 1), [8])]
MLP_PLAN += [(("l1", n), [12 + 10 * n + b for b in (0, 1, 2, 4, 5)]) for n in range(H1 // 128)]
MLP_PLAN += [(("h0", 0), [52]), (("h0", 1), [56])]
MLP_PLAN += [(("l2", n), [60 + 8 * n + b for b in (0, 1, 3, 4)]) for n in range(H2 // 128)] + [(("l3", 0), [76])]
MLP_PARTS = [part for part, _ in MLP_PLAN if part[0] != "h0"]
MLP_LAST = [(("h1", 0), [4]), (("h1", 1), [8])]
MLP_LAST += [(("l1", n), [12 + 7 * n + b for b in range(KB)]) for n in range(H1 // 128)]
MLP_LAST += [(("l2", n), [41 + 7 * n + b for b in range(H1 // 128)]) for n in range(H2 // 128)] + [(("l3", 0), [55])]
MLP_LAST += [(("h0", 0), [58]), (("h0", 1), [61])]
MLP_LAST += [(("s1", 0), [64 + b for b in range(H1 // 128)]), (("s2", 0), [72, 73]), (("s3", 0), [76]), (("turn", 1), [81])]
SOLO_PARTS = [("s1", 0), ("s2", 0), ("s3", 0), ("turn", 1), ("turn0", 1), ("s1", 1), ("s2", 1), ("s3", 1)]

BLOCK0_UNIT = 1 + max(u for u, (_, (p0, pairs, _)) in enumerate(UNITS) if FEATURES + p0 + pairs > 128)
CHUNK_OF = [(PAIRS - 1 - unit[0]) // CHUNK_PAIRS for _, unit in UNITS]


def is_own(part):
    return part[0] == "h0" or part in SOLO_PARTS


def turns_at(u, first_tile=False):
    own = FIRST_TURN_AT if first_tile else TURN_AT
    return [(0, r, half) for r, turns in enumerate(own) for half, p in enumerate(turns) if p == u] + \
        [(1, r, half) for r, turns in enumerate(TURN_AT) for half, p in enumerate(turns) if p == u - UPT]


def keeps_at(u, first_tile=False):
    return (turns_at(0, first_tile) if u == 0 else []) + (turns_at(u + 1, first_tile) if u + 1 < UPT else [])


def highs_at(u, first_tile=False):
    own = FIRST_HIGH_AT if first_tile else HIGH_AT
    return [(0, r) for r, p in enumerate(own) if p == u] + [(1, r) for r, p in enumerate(HIGH_AT) if p == u - UPT]


def share_out():
    shares, backlog = [], 0
    for u, (_, (_, pairs, segments)) in enumerate(UNITS):
        other = len(highs_at(u)) + len(turns_at(u))
        other += sum(units[-1] % UPT == u for part, units in MLP_PLAN) / 2
        a = pairs + 1
        while True:
            a -= 1
            pair = DVE_PAIR / 2 if u in FOLDED else DVE_PAIR
            dve = DVE_OP * (len(segments) + 1) + DVE_PAIR * pairs + pair * (pairs - a)
            now = backlog + ACT_PAIR * a + ACT_COPY * other - dve
            if now <= ACT_BACKLOG or a == 0:
                break
        backlog = max(now, 0)
        shares.append(min(a, pairs - 1))
    return shares


ACT_PAIRS = share_out()
ACT_SUMS = [sum(1 for a in ACT_PAIRS[:u + 1] if a) for u in range(UPT)]
APT = ACT_SUMS[-1]


def tower_kernel(nc, dense_ctx, ids, tables, W1, b1, W2, b2, W3, K, out):
    f32, f32r, i32 = mybir.dt.float32, mybir.dt.float32r, mybir.dt.int32
    ALU = mybir.AluOpType
    ACT = mybir.ActivationFunctionType
    X_AXIS = mybir.AxisListType.X

    ids_v = ids.rearrange("(t p) f -> t p f", p=ROWS)
    dense_v = dense_ctx.rearrange("(t p) c -> t p c", p=ROWS)
    out_v = out.rearrange("(m k p) o -> m p (k o)", k=2, p=ROWS)

    ctx = ExitStack()
    with ctx:
        def sb(name, shape, dt):
            return ctx.enter_context(nc.sbuf_tensor(name, shape, dt))

        def ps(name, cols):
            return ctx.enter_context(nc.psum_tensor(name, [128, cols], f32))

        def sem(name):
            return ctx.enter_context(nc.semaphore(name))

        k_split = sb("k_split", [128, PAIRS * DIM], f32r)
        x = sb("x", [128, 2, FEATURES * DIM], f32)
        x_hi = sb("x_hi", [128, BLOCKS, GF, 2, DIM], f32r)
        x_lo = sb("x_lo", [128, BLOCKS, GF, 2, DIM], f32r)
        xt = sb("xt", [128, XT_SLOTS, GF, 2, ROWS], f32r)
        prod = sb("prod", [128, T_SLOTS, UNIT_COLS], f32)
        h_in = sb("h_in", [128, 2, HIN], f32)
        scratch = sb("scratch", [128, K_SLOTS * CHUNK_COLS], f32)
        hin_t = scratch[:, 0:KB * 256].rearrange("p (k b) -> p k b", k=KB)
        h1_t = scratch[:, KB * 256:KB * 256 + 4 * 256].rearrange("p (k b) -> p k b", k=4)
        h2_t = scratch[:, KB * 256 + 4 * 256:KB * 256 + 6 * 256].rearrange("p (k b) -> p k b", k=2)
        w1 = sb("w1", [128, KB, H1], f32)
        w2 = sb("w2", [128, H1 // 128, H2], f32)
        w3 = sb("w3", [128, H2 // 128], f32)
        bias1 = sb("bias1", [128, H1 // 128], f32)
        bias2 = sb("bias2", [128, H2 // 128], f32)
        ids_sb = sb("ids_sb", [128, 2, FEATURES], i32)
        ident = sb("ident", [128, 128], f32)
        ident_r = sb("ident_r", [128, 128], f32r)
        y_out = sb("y_out", [128, 2], f32)

        y = [ps(f"y{n}", UNIT_COLS) for n in range(Y_SLOTS)]
        x_bank, mlp_bank = ps("x_bank", BANK), ps("mlp_bank", BANK)

        tail_banks = [mlp_bank[:, 0:ROWS], x_bank[:, 0:ROWS], y[0][:, 0:ROWS], y[1][:, 0:ROWS]]
        turn0_bank = y[2][:, 0:ROWS]

        ident_made = sem("ident_made")
        ident_ready = sem("ident_ready")
        k_in = [sem(f"k_in{n}") for n in range(K_SLOTS)]
        k_hi_done = sem("k_hi_done")
        k_ready = sem("k_ready")
        weights_in = sem("weights_in")
        ids_in = [sem(f"ids_in{n}") for n in range(2)]
        gathered = [[sem(f"gathered{k}_{r}") for r in range(GROUPS)] for k in range(2)]
        x_hi_done = sem("x_hi_done")
        first_x_lo_done = sem("first_x_lo_done")
        x_lo_done = sem("x_lo_done")
        xt_filled = sem("xt_filled")
        xt_ready = sem("xt_ready")
        y_ready = sem("y_ready")
        prod_done = sem("prod_done")
        dve_summed = sem("dve_summed")
        act_summed = sem("act_summed")
        folded = sem("folded")
        z_done = sem("z_done")
        dense_in = [sem(f"dense_in{n}") for n in range(2)]
        h0_filled = sem("h0_filled")
        h0_drained = sem("h0_drained")
        mlp_filled = sem("mlp_filled")
        mlp_drained = sem("mlp_drained")
        solo_filled = sem("solo_filled")
        solo_drained = sem("solo_drained")
        tail_filled = sem("tail_filled")
        out_done = sem("out_done")

        block = ctx.enter_context(nc.Block())

        def wait(eng, semaphore, value):
            if not isinstance(value, int) or value > 0:
                eng.wait_ge(semaphore, value)

        def x_lo_of(q):
            if isinstance(q, int) and q <= FIRST_LOWS:
                return first_x_lo_done, q
            return x_lo_done, q - FIRST_LOWS

        def filled(m, part):
            if part[0] == "h0":
                return h0_filled, 2 * m + part[1] + 1
            if part in SOLO_PARTS:
                done = SOLO_PARTS[:SOLO_PARTS.index(part) + 1]
                return solo_filled, sum(p != ("s1", 1) for p in done)
            return mlp_filled, m * len(MLP_PARTS) + MLP_PARTS.index(part) + 1

        def drained(m, part):
            semaphore, value = filled(m, part)
            if semaphore is solo_filled:
                return solo_drained, SOLO_PARTS.index(part) + 1
            return (h0_drained if semaphore is h0_filled else mlp_drained), value

        def turned(m, k):
            return filled(m, (f"h{k}", 1))

        def twice(cols):
            return cols.rearrange("b (f k d) -> b f k d", f=GF, k=1).to_broadcast([128, GF, 2, DIM])

        def pairs_of_tiles(eng, body):
            body(0, True, False)
            with eng.Fori(1, TILES // 2 - 1) as m:
                body(m, False, False)
            body(TILES // 2 - 1, False, True)

        @block.sync
        def _(sp):
            for k in range(2):
                sp.dma_start(ids_sb[:, k, :], ids_v[k]).then_inc(ids_in[k], 16)
            for c in range(CHUNKS):
                if c >= K_SLOTS:
                    sp.wait_ge(k_ready, c - K_SLOTS + 1)
                p0 = PAIRS - (c + 1) * CHUNK_PAIRS
                src = K[p0:p0 + CHUNK_PAIRS].rearrange("p d e -> d p e")
                s = c % K_SLOTS
                dst = scratch[0:DIM, s * CHUNK_COLS:(s + 1) * CHUNK_COLS]
                sp.dma_start(dst.rearrange("d (p e) -> d p e", e=DIM), src).then_inc(k_in[s], 16)
            full = (KB - 1) * 128
            sp.dma_start(w1[:, 0:KB - 1, :], W1[0:full].rearrange("(k p) n -> p k n", p=128)).then_inc(weights_in, 16)
            sp.dma_start(w1[0:KLAST, KB - 1, :], W1[full:HIN]).then_inc(weights_in, 16)
            sp.dma_start(w2[:, :, :], W2.rearrange("(k p) n -> p k n", p=128)).then_inc(weights_in, 16)
            sp.dma_start(w3[:, :], W3.rearrange("(k p) o -> p (k o)", p=128), allow_slow_non_contiguous=True).then_inc(weights_in, 16)
            sp.dma_start(bias1[:, :], b1.rearrange("(k p) -> p k", p=128), allow_slow_non_contiguous=True).then_inc(weights_in, 16)
            sp.dma_start(bias2[:, :], b2.rearrange("(k p) -> p k", p=128), allow_slow_non_contiguous=True).then_inc(weights_in, 16)

            def body(m, first, last):
                for k in range(2):
                    if not first:
                        sp.wait_ge(*turned(m - 1, k))
                    sp.dma_start(h_in[:, k, FEATURES + PAIRS:HIN], dense_v[2 * m + k]).then_inc(dense_in[k], 16)
                    if not last:
                        for r in range(GROUPS):
                            sp.wait_ge(gathered[k][r], (m + 1) * 16 * GF)
                        sp.dma_start(ids_sb[:, k, :], ids_v[2 * m + k + 2]).then_inc(ids_in[k], 16)
                if not first:
                    store(m - 1)

            def store(m, written=("l3", 0)):
                sp.wait_ge(*drained(m, written))
                sp.dma_start(out_v[m], y_out[:, :], allow_slow_non_contiguous=True).then_inc(out_done, 16)

            pairs_of_tiles(sp, body)
            store(TILES // 2 - 1, ("s3", 1))
            sp.wait_ge(out_done, 16 * (TILES // 2))

        @block.gpsimd
        def _(pool):
            nc.gpsimd.memset(ident[:, :], 0.0).then_inc(ident_made, 1)
            pool.wait_ge(ident_made, 1)
            nc.gpsimd.affine_select(out=ident[:, :], in_=ident[:, :], compare_op=ALU.not_equal, fill=1.0,
                                    base=0, pattern=[[-1, 128]], channel_multiplier=1).then_inc(ident_made, 1)

            def gather(k, r, n):
                f = GF * (GROUPS - 1 - r) + n
                nc.gpsimd.indirect_dma_start(
                    x[:, k, f * DIM:(f + 1) * DIM], None, tables[f],
                    bass.IndirectOffsetOnAxis(ap=ids_sb[:, k, f:f + 1], axis=0)).then_inc(gathered[k][r], 16)

            def low_part(m, k, r):
                q = (2 * m + k) * GROUPS + r
                g = GROUPS - 1 - r
                wait(pool, gathered[k][r], (m + 1) * 16 * GF)
                wait(pool, x_hi_done, q + 1)
                wait(pool, xt_filled, 2 * (q + 1 - BLOCKS))
                nc.gpsimd.tensor_tensor(x_lo[:, r % BLOCKS], twice(x[:, k, g * GCOLS:(g + 1) * GCOLS]),
                                        x_hi[:, r % BLOCKS].bitcast(f32), ALU.subtract).then_inc(x_lo_done, 1)

            def x_free(m2, k2):
                wait(pool, ids_in[k2], (m2 + 1) * 16)
                before = 2 * m2 + k2 - 1
                wait(pool, prod_done, before * UPT)
                wait(pool, z_done, before)
                pool.nop(nofuse=True)

            def fold(t, u):
                wait(pool, prod_done, t * UPT + u + 1)
                pairs = prod[:, u % T_SLOTS, 0:(UNITS[u][1][1] - ACT_PAIRS[u]) * DIM].rearrange("b (p e) -> b p e", e=DIM)
                nc.gpsimd.tensor_tensor(pairs[:, :, 0:DIM // 2], pairs[:, :, 0:DIM // 2], pairs[:, :, DIM // 2:DIM],
                                        ALU.add).then_inc(folded, 1)

            def tile(m, k, m2, k2, first, last):
                for u in range(UPT):
                    for r in range(GROUPS):
                        if LOW_AT[r] == u and not (first and r < GROUPS - 1):
                            low_part(m, k, r)
                        if LOW_AT[r] + UPT == u and not last:
                            low_part(m2, k2, r)
                    if u == 0 and not last:
                        x_free(m2, k2)
                    if not last:
                        for n in range(u * FEATURES // (UPT - 1), min((u + 1) * FEATURES // (UPT - 1), FEATURES)):
                            gather(k2, n // GF, n % GF)
                    if u in (FIRST_FOLDED if first else LAST_FOLDED if last else FOLDED):
                        fold(2 * m + k, u)

            pool.wait_ge(ids_in[0], 16)
            for r in range(GROUPS):
                for n in range(GF):
                    gather(0, r, n)
                if r > FIRST_LOWS:
                    low_part(0, 0, r - 1)

            def body(m, first, last):
                tile(m, 0, m, 1, first, False)
                tile(m, 1, m + 1, 0, False, last)

            pairs_of_tiles(pool, body)

        @block.tensor
        def _(pe):
            def transpose_x(m, k, r, half):
                q = (2 * m + k) * GROUPS + r
                wait(pe, *x_lo_of(q + 1))
                wait(pe, xt_ready, 2 * q + half)
                for f in range(2):
                    for n, part in enumerate((x_hi, x_lo)):
                        place = (2 * f + n) * ROWS
                        last = nc.tensor.matmul(x_bank[:, place:place + ROWS],
                                                part[:, r % BLOCKS, 2 * half + f].rearrange("b k d -> b (k d)"),
                                                ident_r[:, :], start=True, stop=True)
                last.then_inc(xt_filled, 1)

            def make_y(m, k, u, first):
                t = 2 * m + k
                r, (p0, pairs, segments) = UNITS[u]
                if u == FIRST_UNIT[r]:
                    wait(pe, xt_ready, 2 * (t * GROUPS + r + 1))
                if first and k == 0:
                    pe.wait_ge(k_ready, CHUNK_OF[u] + 1)
                wait(pe, prod_done, t * UPT + u + 1 - Y_SLOTS)
                dst = y[u % Y_SLOTS]
                for i, _, count, place in segments:
                    cuts = [place] + [c for c in (BANK_PAIRS,) if place < c < place + count] + [place + count]
                    for part in range(2):
                        for a, b in zip(cuts, cuts[1:]):
                            last = nc.tensor.matmul(
                                dst[:, a * DIM:b * DIM], xt[:, r % XT_SLOTS, i % GF, part, :],
                                k_split[:, (p0 + a) * DIM:(p0 + b) * DIM], start=part == 0, stop=part == 1)
                last.then_inc(y_ready, 1)

            def layer1(dst, k, n, block, start, stop):
                rows = 128 if block < KB - 1 else KLAST
                return nc.tensor.matmul(dst, w1[0:rows, block, n * 128:(n + 1) * 128],
                                        hin_t[0:rows, block, k * ROWS:(k + 1) * ROWS], start=start, stop=stop)

            def mlp_step(m, part, b, before):
                kind, n = part
                last_one = True
                if b == 0 and before:
                    pe.wait_ge(*drained(*before))
                if kind in ("h0", "h1"):
                    k = int(kind[1])
                    if n == 0:
                        t = 2 * m + k
                        wait(pe, dve_summed, (t + 1) * UPT)
                        wait(pe, act_summed, (t + 1) * APT)
                        wait(pe, z_done, t + 1)
                        wait(pe, dense_in[k], (m + 1) * 16)
                    for j in range(KB - 1) if n == 0 else [KB - 1]:
                        cols = slice(j * 128, min((j + 1) * 128, HIN))
                        place = j % (KB - 1) * ROWS
                        done = nc.tensor.transpose(mlp_bank[0:cols.stop - cols.start, place:place + ROWS],
                                                   h_in[:, k, cols], ident[:, :])
                elif kind == "turn":
                    t = 2 * m + 1
                    pe.wait_ge(dve_summed, t * UPT + BLOCK0_UNIT)
                    pe.wait_ge(act_summed, t * APT + ACT_SUMS[BLOCK0_UNIT - 1])
                    pe.wait_ge(dense_in[1], (m + 1) * 16)
                    for j in range(1, KB):
                        cols = slice(j * 128, min((j + 1) * 128, HIN))
                        done = nc.tensor.transpose(mlp_bank[0:cols.stop - cols.start, (j - 1) * ROWS:j * ROWS],
                                                   h_in[:, 1, cols], ident[:, :])
                elif kind == "turn0":
                    pe.wait_ge(dve_summed, (2 * m + 2) * UPT)
                    pe.wait_ge(act_summed, (2 * m + 2) * APT)
                    pe.wait_ge(z_done, 2 * m + 2)
                    done = nc.tensor.transpose(turn0_bank, h_in[:, 1, 0:128], ident[:, :])
                elif kind == "s1":
                    if b == 0:
                        pe.wait_ge(*drained(m, ("h0", 1)))
                    last_one = b == H1 // 128 - 1
                    for block in range(KB):
                        done = layer1(mlp_bank[:, b * ROWS:(b + 1) * ROWS], 0, b, block, block == 0, block == KB - 1)
                elif kind == "s2":
                    k = n
                    if k or b == 0:
                        pe.wait_ge(*drained(m, ("s1", k)))
                    last_one = k or b == H2 // 128 - 1
                    for c in range(H2 // 128) if k else [b]:
                        for j in range(H1 // 128):
                            done = nc.tensor.matmul(mlp_bank[:, c * ROWS:(c + 1) * ROWS], w2[:, j, c * 128:(c + 1) * 128],
                                                    h1_t[:, j, k * ROWS:(k + 1) * ROWS],
                                                    start=j == 0, stop=j == H1 // 128 - 1)
                elif kind == "s3":
                    k = n
                    pe.wait_ge(*drained(m, ("s2", k)))
                    for j in range(H2 // 128):
                        done = nc.tensor.matmul(mlp_bank[:, 0:1], h2_t[:, j, k * ROWS:(k + 1) * ROWS],
                                                w3[:, j:j + 1], start=j == 0, stop=j == H2 // 128 - 1)
                elif kind == "l1":
                    if n == 0 and b == 0:
                        pe.wait_ge(*drained(m, ("h1", 1)))
                    rows = 128 if b < KB - 1 else KLAST
                    last_one = b == KB - 1
                    done = nc.tensor.matmul(mlp_bank[:, 0:256], w1[0:rows, b, n * 128:(n + 1) * 128],
                                            hin_t[0:rows, b, :], start=b == 0, stop=last_one)
                elif kind == "l2":
                    if n == 0 and b == 0:
                        pe.wait_ge(*drained(m, ("l1", H1 // 128 - 1)))
                    last_one = b == H1 // 128 - 1
                    done = nc.tensor.matmul(mlp_bank[:, 0:256], w2[:, b, n * 128:(n + 1) * 128],
                                            h1_t[:, b, :], start=b == 0, stop=last_one)
                else:
                    pe.wait_ge(*drained(m, ("l2", H2 // 128 - 1)))
                    for k in range(2):
                        for j in range(H2 // 128):
                            done = nc.tensor.matmul(mlp_bank[:, k:k + 1], h2_t[:, j, k * ROWS:(k + 1) * ROWS],
                                                    w3[:, j:j + 1], start=j == 0, stop=j == H2 // 128 - 1)
                if last_one:
                    done.then_inc(filled(m, part)[0], 1)

            def body(m, first, last):
                before = None if first else (m - 1, ("h0", 1))
                for k in range(2):
                    for u in range(UPT):
                        for ahead, r, half in turns_at(u, first and k == 0):
                            if not (last and k and ahead):
                                transpose_x(m + (k + ahead) // 2, (k + ahead) % 2, r, half)
                        for part, units in MLP_LAST if last else MLP_PLAN:
                            own = is_own(part)
                            if k * UPT + u in units and (own or not first):
                                mlp_step(m if own else m - 1, part, units.index(k * UPT + u), before)
                                if k * UPT + u == units[-1]:
                                    before = (m if own else m - 1, part)
                        make_y(m, k, u, first)

            pe.wait_ge(ident_ready, 1)
            for half in range(2):
                transpose_x(0, 0, 0, half)
            pe.wait_ge(ident_made, 2)
            body(0, True, False)
            pe.wait_ge(weights_in, 6 * 16)
            with pe.Fori(1, TILES // 2 - 1) as m:
                body(m, False, False)
            m = TILES // 2 - 1
            body(m, False, True)
            pe.wait_ge(*drained(m, ("turn", 1)))
            for n, dst in enumerate(tail_banks):
                if n == 1:
                    pe.wait_ge(xt_ready, 2 * TILES * GROUPS)
                if n > 1:
                    pe.wait_ge(prod_done, TILES * UPT - Y_SLOTS + n - 1)
                for block in range(1, KB):
                    layer1(dst, 1, n, block, block == 1, False)
            mlp_step(m, ("turn0", 1), 0, None)
            pe.wait_ge(*drained(m, ("turn0", 1)))
            for n, dst in enumerate(tail_banks):
                layer1(dst, 1, n, 0, False, True).then_inc(tail_filled, 1)
            mlp_step(m, ("s2", 1), 0, (m, ("s1", 1)))
            mlp_step(m, ("s3", 1), 0, (m, ("s2", 1)))

        @block.vector
        def _(dve):
            dve.wait_ge(ident_made, 2)
            nc.vector.tensor_copy(ident_r[:, :], ident[:, :]).then_inc(ident_ready, 1)
            split = [0]

            def split_k(upto):
                while split[0] <= min(upto, CHUNKS - 1):
                    c = split[0]
                    split[0] += 1
                    p0 = PAIRS - (c + 1) * CHUNK_PAIRS
                    cols = slice(p0 * DIM, p0 * DIM + CHUNK_COLS)
                    s = c % K_SLOTS
                    dve.wait_ge(k_hi_done, c + 1)
                    nc.vector.tensor_tensor(k_split[DIM:128, cols], scratch[0:DIM, s * CHUNK_COLS:(s + 1) * CHUNK_COLS],
                                            k_split[0:DIM, cols].bitcast(f32), ALU.subtract).then_inc(k_ready, 1)

            def sum_unit(t, k, u, fold_plan):
                p0, pairs, _ = UNITS[u][1]
                mine = pairs - ACT_PAIRS[u]
                dve.wait_ge(prod_done, t * UPT + u + 1)
                width = DIM
                if u in fold_plan:
                    width = DIM // 2
                    before = 0 if fold_plan is FIRST_FOLDED else len(FIRST_FOLDED) + (t - 1) * FPT
                    dve.wait_ge(folded, before + fold_plan.index(u) + 1)
                nc.vector.tensor_reduce(
                    h_in[:, k, FEATURES + p0:FEATURES + p0 + mine],
                    prod[:, u % T_SLOTS, 0:mine * DIM].rearrange("b (p e) -> b p e", e=DIM)[:, :, 0:width],
                    X_AXIS, ALU.add).then_inc(dve_summed, 1)

            def first_low(r):
                g = GROUPS - 1 - r
                dve.wait_ge(gathered[0][r], 16 * GF)
                dve.wait_ge(x_hi_done, r + 1)
                wait(dve, xt_filled, 2 * (r + 1 - BLOCKS))
                nc.vector.tensor_tensor(x_lo[:, r % BLOCKS], twice(x[:, 0, g * GCOLS:(g + 1) * GCOLS]),
                                        x_hi[:, r % BLOCKS].bitcast(f32), ALU.subtract).then_inc(first_x_lo_done, 1)

            def body(m, first, last):
                for k in range(2):
                    t = 2 * m + k
                    last_tile = last and k == 1
                    fold_plan = FIRST_FOLDED if first and k == 0 else LAST_FOLDED if last_tile else FOLDED
                    late = [] if last_tile else fold_plan
                    if not first:
                        dve.wait_ge(*turned(m - 1, k))
                    for u, (r, (p0, pairs, segments)) in enumerate(UNITS):
                        if first and k == 0:
                            if u in FIRST_LOWS_AT:
                                first_low(FIRST_LOWS_AT.index(u))
                            split_k(CHUNK_OF[min(u + K_AHEAD, UPT - 1)])
                        if u == FIRST_UNIT[r]:
                            dve.wait_ge(gathered[k][r], (m + 1) * 16 * GF)
                        dve.wait_ge(y_ready, t * UPT + u + 1)
                        before = u - T_SLOTS
                        wait(dve, act_summed, t * APT + ACT_SUMS[before] if before >= 0
                             else (t - 1) * APT + ACT_SUMS[before + UPT])
                        wait(dve, dve_summed, t * UPT + before + 1)
                        for n, (i, j, count, place) in enumerate(segments):
                            cols = slice(place * DIM, (place + count) * DIM)
                            done = nc.vector.tensor_tensor(prod[:, u % T_SLOTS, cols], y[u % Y_SLOTS][:, cols],
                                                           x[:, k, j * DIM:(j + count) * DIM], ALU.mult)
                        done.then_inc(prod_done, 1)
                        if u > 1 and u - 2 in late:
                            sum_unit(t, k, u - 2, fold_plan)
                        if u and u - 1 not in late:
                            sum_unit(t, k, u - 1, fold_plan)
                    nc.vector.tensor_reduce(h_in[:, k, 0:FEATURES], x[:, k, :].rearrange("b (f e) -> b f e", e=DIM),
                                            X_AXIS, ALU.add).then_inc(z_done, 1)
                    if UPT - 2 in late:
                        sum_unit(t, k, UPT - 2, fold_plan)
                    sum_unit(t, k, UPT - 1, fold_plan)

            split_k(3)
            first_low(0)
            split_k(4)
            first_low(1)
            pairs_of_tiles(dve, body)

        @block.scalar
        def _(act):
            split = [0]

            def split_k(upto):
                while split[0] <= min(upto, CHUNKS - 1):
                    c = split[0]
                    split[0] += 1
                    p0 = PAIRS - (c + 1) * CHUNK_PAIRS
                    s = c % K_SLOTS
                    act.wait_ge(k_in[s], (c // K_SLOTS + 1) * 16)
                    nc.scalar.activation(k_split[0:DIM, p0 * DIM:p0 * DIM + CHUNK_COLS],
                                         scratch[0:DIM, s * CHUNK_COLS:(s + 1) * CHUNK_COLS], ACT.Copy)\
                        .then_inc(k_hi_done, 1)

            def high_part(m, k, r):
                q = (2 * m + k) * GROUPS + r
                g = GROUPS - 1 - r
                wait(act, gathered[k][r], (m + 1) * 16 * GF)
                wait(act, xt_filled, 2 * (q + 1 - BLOCKS))
                wait(act, *x_lo_of(q + 1 - BLOCKS))
                nc.scalar.activation(x_hi[:, r % BLOCKS], twice(x[:, k, g * GCOLS:(g + 1) * GCOLS]), ACT.Copy)\
                    .then_inc(x_hi_done, 1)

            def keep_x(m, k, r, half):
                wait(act, xt_filled, 2 * ((2 * m + k) * GROUPS + r) + half + 1)
                nc.scalar.activation(xt[:, r % XT_SLOTS, 2 * half:2 * half + 2].rearrange("p f n b -> p (f n b)"),
                                     x_bank[:, :], ACT.Copy).then_inc(xt_ready, 1)

            def sum_unit(m, k, u, first):
                if first and k == 0:
                    split_k(CHUNK_OF[min(u + 2 + K_AHEAD, UPT - 1)])
                if not ACT_PAIRS[u]:
                    return
                p0, pairs, _ = UNITS[u][1]
                act.wait_ge(prod_done, (2 * m + k) * UPT + u + 1)
                for p in range(pairs - ACT_PAIRS[u], pairs):
                    cols = prod[:, u % T_SLOTS, p * DIM:(p + 1) * DIM]
                    done = nc.scalar.activation(cols, cols, ACT.Copy,
                                                accum_out=h_in[:, k, FEATURES + p0 + p:FEATURES + p0 + p + 1])
                done.then_inc(act_summed, 1)

            def mlp_out(m, part):
                kind, n = part
                if part != ("s1", 1):
                    act.wait_ge(*filled(m, part))
                if kind in ("h0", "h1"):
                    cols = slice(int(kind[1]) * ROWS, int(kind[1]) * ROWS + ROWS)
                    if n == 0:
                        done = nc.scalar.activation(hin_t[:, 0:KB - 1, cols],
                                                    mlp_bank[:, :].rearrange("p (b c) -> p b c", b=KB - 1), ACT.Copy)
                    else:
                        done = nc.scalar.activation(hin_t[0:KLAST, KB - 1, cols], mlp_bank[0:KLAST, 0:ROWS], ACT.Copy)
                elif kind == "turn":
                    done = nc.scalar.activation(hin_t[:, 1:KB, ROWS:2 * ROWS],
                                                mlp_bank[:, :].rearrange("p (b c) -> p b c", b=KB - 1), ACT.Copy)
                elif kind == "turn0":
                    done = nc.scalar.activation(hin_t[:, 0, ROWS:2 * ROWS], turn0_bank, ACT.Copy)
                elif kind == "s1":
                    for j in range(H1 // 128):
                        if n:
                            act.wait_ge(tail_filled, j + 1)
                        done = nc.scalar.activation(h1_t[:, j, n * ROWS:(n + 1) * ROWS],
                                                    tail_banks[j] if n else mlp_bank[:, j * ROWS:(j + 1) * ROWS],
                                                    ACT.Relu, bias=bias1[:, j:j + 1])
                elif kind == "s2":
                    for j in range(H2 // 128):
                        done = nc.scalar.activation(h2_t[:, j, n * ROWS:(n + 1) * ROWS],
                                                    mlp_bank[:, j * ROWS:(j + 1) * ROWS], ACT.Relu, bias=bias2[:, j:j + 1])
                elif kind == "s3":
                    if n == 0:
                        act.wait_ge(out_done, m * 16)
                    done = nc.scalar.activation(y_out[:, n:n + 1], mlp_bank[:, 0:1], ACT.Copy)
                elif kind == "l1":
                    done = nc.scalar.activation(h1_t[:, n, :], mlp_bank[:, 0:256], ACT.Relu, bias=bias1[:, n:n + 1])
                elif kind == "l2":
                    done = nc.scalar.activation(h2_t[:, n, :], mlp_bank[:, 0:256], ACT.Relu, bias=bias2[:, n:n + 1])
                else:
                    wait(act, out_done, m * 16)
                    done = nc.scalar.activation(y_out[:, :], mlp_bank[:, 0:2], ACT.Copy)
                done.then_inc(drained(m, part)[0], 1)

            def body(m, first, last):
                for k in range(2):
                    for u in range(UPT):
                        for ahead, r in highs_at(u, first and k == 0):
                            if not (last and k and ahead):
                                high_part(m + (k + ahead) // 2, (k + ahead) % 2, r)
                        for ahead, r, half in keeps_at(u, first and k == 0):
                            if not (last and k and ahead):
                                keep_x(m + (k + ahead) // 2, (k + ahead) % 2, r, half)
                        for part, units in MLP_LAST if last else MLP_PLAN:
                            own = is_own(part)
                            if units[-1] == k * UPT + u and (own or not first):
                                mlp_out(m if own else m - 1, part)
                        if u == 0 and not first:
                            act.wait_ge(*turned(m - 1, k))
                        sum_unit(m, k, u, first)

            split_k(3)
            high_part(0, 0, 0)
            split_k(4)
            keep_x(0, 0, 0, 0)
            high_part(0, 0, 1)
            keep_x(0, 0, 0, 1)
            split_k(5)
            body(0, True, False)
            act.wait_ge(weights_in, 6 * 16)
            with act.Fori(1, TILES // 2 - 1) as m:
                body(m, False, False)
            m = TILES // 2 - 1
            body(m, False, True)
            for part in SOLO_PARTS[SOLO_PARTS.index(("turn0", 1)):]:
                mlp_out(m, part)


_INS = ["dense_ctx", "ids"] + [f"tbl_{f}" for f in range(32)] + ["W_top1", "b_top1", "W_top2", "b_top2", "W_top3",
                                                                "L0_rec_kernels"]
_OUT = ((1024, 1), "float32")


def kernel(**inputs):
    import numpy as _np
    import concourse.bacc as _bacc
    from concourse import mybir as _mybir
    from concourse.bass_utils import run_bass_kernel_spmd as _run

    nc = _bacc.Bacc("TRN2", target_bir_lowering=False, num_devices=1)
    arrays, args = {}, {}
    for name in _INS:
        a = _np.ascontiguousarray(inputs[name])
        arrays[f"in_{name}_dram"] = a
        args[name] = nc.dram_tensor(f"in_{name}_dram", a.shape, _mybir.dt.from_np(a.dtype), kind="ExternalInput").ap()
    out = nc.dram_tensor("out_0_dram", _OUT[0], _mybir.dt.from_np(_np.dtype(_OUT[1])), kind="ExternalOutput").ap()
    tower_kernel(nc, args["dense_ctx"], args["ids"], [args[f"tbl_{f}"] for f in range(32)], args["W_top1"],
                 args["b_top1"], args["W_top2"], args["b_top2"], args["W_top3"], args["L0_rec_kernels"], out)
    r = _run(nc, [arrays], core_ids=[0])
    return r.results[0]["out_0_dram"]
```
